# Optimizing a Trainium2 kernel written in Bass

```python
import numpy as np
import jax
import jax.numpy as jnp

def _softmax(x, axis=-1):
    return jax.nn.softmax(x, axis=axis)

def _gelu(x):
    return jax.nn.gelu(x, approximate=True)

def _silu(x):
    return jax.nn.silu(x)

def _sigmoid(x):
    return jax.nn.sigmoid(x)

def _layernorm(x, axis=-1, eps=1e-05):
    m = jnp.mean(x, axis=axis, keepdims=True)
    v = jnp.var(x, axis=axis, keepdims=True)
    return (x - m) / jnp.sqrt(v + eps)

def _scatter_add(tgt, idx, src, axis=0):
    return tgt.at[idx].add(src)

def _segment_sum(src, seg, n):
    return jax.ops.segment_sum(src, seg, n)
kernel_name = 'mk_seq_preln_d1_jaxref_r4_1765f0'

def setup_inputs(seed: int=0):
    np.random.seed(seed)
    _w = jnp.asarray

    def _L0_attn_setup():
        import jax, jax.numpy as jnp
        import numpy as np
        H = 256
        W_CTX = 2

        def _local_attention(x, Wq, bq, Wk, bk, Wv, bv):
            B, S, Hd = x.shape
            Q = x @ Wq + bq
            K = x @ Wk + bk
            V = x @ Wv + bv
            w = W_CTX
            win = 2 * w + 1
            idx = jnp.arange(S)[:, None] + jnp.arange(-w, w + 1)[None, :]
            valid = (idx >= 0) & (idx < S)
            idx_c = jnp.clip(idx, 0, S - 1)
            Kw = K[:, idx_c]
            Vw = V[:, idx_c]
            scores = jnp.einsum('bsh,bswh->bsw', Q, Kw) / jnp.sqrt(jnp.float32(Hd))
            scores = jnp.where(valid[None], scores, -jnp.inf)
            probs = jax.nn.softmax(scores, axis=-1)
            return jnp.einsum('bsw,bswh->bsh', probs, Vw)
        key = jax.random.key(seed)
        ks = jax.random.split(key, 7)
        B, S = (4, 512)
        sd = 1.0 / np.sqrt(H)
        inp = {'sequence_output': jax.random.normal(ks[0], (B, S, H), dtype=jnp.float32), 'Wq': jax.random.uniform(ks[1], (H, H), jnp.float32, -sd, sd), 'bq': jax.random.uniform(ks[2], (H,), jnp.float32, -sd, sd), 'Wk': jax.random.uniform(ks[3], (H, H), jnp.float32, -sd, sd), 'bk': jax.random.uniform(ks[4], (H,), jnp.float32, -sd, sd), 'Wv': jax.random.uniform(ks[5], (H, H), jnp.float32, -sd, sd), 'bv': jax.random.uniform(ks[6], (H,), jnp.float32, -sd, sd)}
        return inp
    _L0_attn_in = _L0_attn_setup()

    def _L0_ffn_setup():
        import jax, jax.numpy as jnp
        import numpy as np
        B, S, H = (2, 256, 256)
        KD, NH, K = (128, 8, 8)
        NE = 16384
        NK = 64
        EPS = 1e-05
        key = jax.random.key(seed)
        ks = jax.random.split(key, 5)
        inputs = jax.random.normal(ks[0], (B, S, H), jnp.float32)
        bn_gamma = jnp.ones((H,), jnp.float32)
        bn_beta = jnp.zeros((H,), jnp.float32)
        w_q = jax.random.normal(ks[1], (2 * NH * KD, H), jnp.float32) * (1.0 / np.sqrt(H))
        keys_p = jax.random.normal(ks[2], (NH, NK, 2, KD), jnp.float32) * 0.02
        lim = float(np.sqrt(6.0 / (NE + H)))
        down = jax.random.uniform(ks[3], (NE, H), jnp.float32, -lim, lim)
        up = jax.random.uniform(ks[4], (NE, H), jnp.float32, -lim, lim)
        return {'inputs': inputs, 'bn_gamma': bn_gamma, 'bn_beta': bn_beta, 'w_q': w_q, 'keys_p': keys_p, 'down': down, 'up': up}
    _L0_ffn_in = _L0_ffn_setup()
    _d = {'L0_attn_sequence_output': _L0_attn_in['sequence_output'], 'L0_attn_Wq': _L0_attn_in['Wq'], 'L0_attn_bq': _L0_attn_in['bq'], 'L0_attn_Wk': _L0_attn_in['Wk'], 'L0_attn_bk': _L0_attn_in['bk'], 'L0_attn_Wv': _L0_attn_in['Wv'], 'L0_attn_bv': _L0_attn_in['bv'], 'L0_ffn_bn_gamma': _L0_ffn_in['bn_gamma'], 'L0_ffn_bn_beta': _L0_ffn_in['bn_beta'], 'L0_ffn_w_q': _L0_ffn_in['w_q'], 'L0_ffn_keys_p': _L0_ffn_in['keys_p'], 'L0_ffn_down': _L0_ffn_in['down'], 'L0_ffn_up': _L0_ffn_in['up']}
    _x0 = _d['L0_attn_sequence_output']
    _d['L0_attn_sequence_output'] = jax.random.normal(jax.random.fold_in(jax.random.key(seed), 1), (2, 4096, 256), dtype=_x0.dtype)
    del _x0
    return _d

def reference(L0_attn_sequence_output, L0_attn_Wq, L0_attn_bq, L0_attn_Wk, L0_attn_bk, L0_attn_Wv, L0_attn_bv, L0_ffn_bn_gamma, L0_ffn_bn_beta, L0_ffn_w_q, L0_ffn_keys_p, L0_ffn_down, L0_ffn_up):

    def _L0_attn_ref(sequence_output, Wq, bq, Wk, bk, Wv, bv):
        import jax, jax.numpy as jnp
        import numpy as np
        H = 256
        W_CTX = 2

        def _local_attention(x, Wq, bq, Wk, bk, Wv, bv):
            B, S, Hd = x.shape
            Q = x @ Wq + bq
            K = x @ Wk + bk
            V = x @ Wv + bv
            w = W_CTX
            win = 2 * w + 1
            idx = jnp.arange(S)[:, None] + jnp.arange(-w, w + 1)[None, :]
            valid = (idx >= 0) & (idx < S)
            idx_c = jnp.clip(idx, 0, S - 1)
            Kw = K[:, idx_c]
            Vw = V[:, idx_c]
            scores = jnp.einsum('bsh,bswh->bsw', Q, Kw) / jnp.sqrt(jnp.float32(Hd))
            scores = jnp.where(valid[None], scores, -jnp.inf)
            probs = jax.nn.softmax(scores, axis=-1)
            return jnp.einsum('bsw,bswh->bsh', probs, Vw)
        return _local_attention(sequence_output, Wq, bq, Wk, bk, Wv, bv)

    def _L0_ffn_ref(inputs, bn_gamma, bn_beta, w_q, keys_p, down, up):
        import jax, jax.numpy as jnp
        import numpy as np
        B, S, H = (2, 256, 256)
        KD, NH, K = (128, 8, 8)
        NE = 16384
        NK = 64
        EPS = 1e-05
        b, s, d = inputs.shape
        x = inputs.reshape(b * s, d)
        mean = x.mean(axis=0)
        var = x.var(axis=0)
        xn = (x - mean) * jax.lax.rsqrt(var + EPS) * bn_gamma + bn_beta
        xn = xn.reshape(b, s, d)
        q = (xn @ w_q.T).reshape(b, s, 2, NH, KD).transpose(2, 0, 1, 3, 4)
        sim = jnp.einsum('pbnhd,hkpd->pbnhk', q, keys_p)
        scores, idx = jax.lax.top_k(sim, K)
        all_scores = (scores[0][..., :, None] + scores[1][..., None, :]).reshape(b, s, NH, K * K)
        all_idx = (idx[0][..., :, None] * NK + idx[1][..., None, :]).reshape(b, s, NH, K * K)
        sc, pk = jax.lax.top_k(all_scores, K)
        indices = jnp.take_along_axis(all_idx, pk, axis=-1)
        wd = down[indices]
        hmid = jnp.einsum('bnd,bnhkd->bnhk', inputs, wd)
        hmid = jax.nn.sigmoid(sc) * jax.nn.gelu(hmid, approximate=False)
        wu = up[indices]
        return jnp.einsum('bnhk,bnhkd->bnd', hmid, wu)
    x = L0_attn_sequence_output
    x = x + _L0_attn_ref(_layernorm(x, axis=-1), L0_attn_Wq, L0_attn_bq, L0_attn_Wk, L0_attn_bk, L0_attn_Wv, L0_attn_bv)
    x = x + _L0_ffn_ref(_layernorm(x, axis=-1), L0_ffn_bn_gamma, L0_ffn_bn_beta, L0_ffn_w_q, L0_ffn_keys_p, L0_ffn_down, L0_ffn_up)
    return x

_drawn_inputs = setup_inputs


def setup_inputs(seed=0):
    import zlib

    import numpy as np

    out = dict(_drawn_inputs(seed))
    spreads = {'L0_ffn_bn_gamma': (1.0, 0.6), 'L0_ffn_bn_beta': (0.0, 0.8)}
    factors = {'L0_attn_bq': 8.0,
     'L0_attn_bk': 8.0,
     'L0_ffn_w_q': 8.0,
     'L0_ffn_keys_p': 8.0,
     'L0_ffn_down': 8.0,
     'L0_ffn_up': 8.0}
    for name, (base, spread) in spreads.items():
        noise = np.random.default_rng([zlib.crc32(name.encode()), seed]).standard_normal(out[name].shape)
        drawn = base * np.exp(spread * noise) if base else spread * noise
        out[name] = jnp.asarray(drawn.astype(out[name].dtype))
    for name, factor in factors.items():
        out[name] = (out[name] * factor).astype(out[name].dtype)
    return out
```

```python
import concourse.bass as bass
from concourse import mybir
from contextlib import ExitStack



def window_attention_peer_kernel(
    nc: bass.Bass,
    x: bass.AP,
    wq: bass.AP,
    bq: bass.AP,
    wk: bass.AP,
    bk: bass.AP,
    wv: bass.AP,
    bv: bass.AP,
    gamma: bass.AP,
    beta: bass.AP,
    w_query: bass.AP,
    keys_t: bass.AP,
    table: bass.AP,
    out: bass.AP,
):
    f32 = mybir.dt.float32
    u32 = mybir.dt.uint32
    ALU = mybir.AluOpType
    ACT = mybir.ActivationFunctionType
    AX = mybir.AxisListType

    P = 128
    NB, S, H = x.shape
    HC = H // P
    W = 2
    QS = P - 2 * W
    STEPS = (S - P) // QS + 1
    assert (STEPS - 1) * QS + P == S
    SCALE = float(H) ** -0.5
    EPS = 1e-5
    FAR = -1.0e30
    NH = 8
    K = 8
    NK = keys_t.shape[2]
    UNITS = 2 * NH
    TOKENS = NB * S
    TILES = TOKENS // P

    ctx = ExitStack()
    with ctx:
        def sb(name, shape, dt=f32):
            return ctx.enter_context(nc.sbuf_tensor(name, shape, dt))

        def sem(name):
            return ctx.enter_context(nc.semaphore(name))

        x_s = x.rearrange("b s d -> s b d")
        x2_d = nc.dram_tensor("x2_scratch", (NB, S, H), f32, kind="Internal").ap()
        ln2_d = nc.dram_tensor("ln2_scratch", (NB, S, H), f32, kind="Internal").ap()
        x2_s = x2_d.rearrange("b s d -> s b d")
        ln2_s = ln2_d.rearrange("b s d -> s b d")
        x2_t = x2_d.rearrange("b s d -> (b s) d")
        ln2_t = ln2_d.rearrange("b s d -> (b s) d")
        out_t = out.rearrange("b s d -> (b s) d")

        ident = sb("ident", [P, P])
        half_ident = sb("half_ident", [P, P])
        band = sb("band", [P, P])
        valid = sb("valid", [P, 3])
        iota8 = sb("iota8", [P, K])
        ones_row = sb("ones_row", [1, P])
        wq_sb = sb("wq_sb", [P, HC, H])
        wk_sb = sb("wk_sb", [P, HC, H])
        wv_sb = sb("wv_sb", [P, HC, H])
        bq_sb = sb("bq_sb", [P, HC])
        bk_sb = sb("bk_sb", [P, HC])
        bv_sb = sb("bv_sb", [P, H])
        gamma_sb = sb("gamma_sb", [P, HC])
        beta_sb = sb("beta_sb", [P, HC])
        fold = sb("fold", [P, HC, UNITS * NK])
        fold_n = sb("fold_n", [P, HC, UNITS * NK])
        fold_b = sb("fold_b", [1, UNITS * NK])

        rows = sb("rows", [P, NH, K, 2 * H])
        flat = rows[:, :, :, :].rearrange("p a b c -> p (a b c)")
        spot = [0]

        def shared(*dims):
            n = 1
            for d in dims:
                n *= d
            v = flat[:, spot[0]:spot[0] + n]
            spot[0] += n
            assert spot[0] <= NH * K * 2 * H
            names = "abcd"[:len(dims)]
            if len(dims) == 1:
                return v
            return v.rearrange(f"p ({' '.join(names)}) -> p {' '.join(names)}",
                               **{c: d for c, d in zip(names, dims)})

        wquery_sb = shared(UNITS, H)
        keys_sb = shared(UNITS, NK)
        xa = [shared(NB, H) for _ in range(2)]
        xr = [shared(NB, H) for _ in range(2)]
        ln = shared(NB, H)
        lnT = shared(HC, NB, P)
        qT = shared(HC, NB * P)
        kT = shared(HC, NB * P)
        v_sb = [shared(NB, H) for _ in range(2)]
        sm = shared(NB, P)
        pr = shared(NB, P)
        prT = shared(NB, P)
        x2 = [shared(NB, H) for _ in range(2)]
        ln2 = [shared(NB, H) for _ in range(2)]
        sq = shared(NB, H)
        acc = shared(3, 2, NB * H)
        bst = sb("bst", [P, 4, 6])
        mv = sb("mv", [P, 4, 2])
        veps = sb("veps", [P, 4])
        lnv = sb("lnv", [P, 4])
        y0 = sb("y0", [P, 4])
        y2 = sb("y2", [P, 4])
        y3 = sb("y3", [P, 4])
        y4 = sb("y4", [P, 4])
        rstd = sb("rstd", [P, 4])
        nmax = sb("nmax", [P, NB])
        rsum = [sb(f"rsum{i}", [P, NB]) for i in range(2)]
        rcp = sb("rcp", [P, NB])
        bs = sb("bs", [P, 12, HC])

        lnb = [sb(f"lnb{i}", [P, H]) for i in range(2)]
        xres = [sb(f"xres{i}", [P, H]) for i in range(2)]
        lnbT = sb("lnbT", [P, HC, P])
        top = sb("top", [P, UNITS, K])
        topi = sb("topi", [P, UNITS, K], u32)
        pair = sb("pair", [P, NH, K * K])
        best = sb("best", [P, NH, K])
        besti = sb("besti", [P, NH * K], u32)
        pos = sb("pos", [P, 2, NH * K], u32)
        hot = sb("hot", [P, 2, NH * K, K])
        hotv = sb("hotv", [P, 2, NH * K, K])
        part = sb("part", [P, 2, NH * K])
        idx = [sb(f"idx{i}", [P, NH * K], u32) for i in range(2)]
        tanh = [sb(f"tanh{i}", [P, NH * K]) for i in range(2)]
        hid = [sb(f"hid{i}", [P, NH * K]) for i in range(2)]
        gel = [sb(f"gel{i}", [P, NH * K]) for i in range(2)]
        coef = [sb(f"coef{i}", [P, NH * K]) for i in range(2)]
        diag = [sb(f"diag{i}", [P, K, P]) for i in range(2)]
        outb = [sb(f"outb{i}", [P, H]) for i in range(2)]

        bank = [ctx.enter_context(nc.psum_tensor(f"bank{i}", [P, 512], f32)) for i in range(8)]
        ps_t = bank[0][:, :].rearrange("p (c b t) -> p c b t", c=HC, b=NB)
        ps_q = bank[1][:, :].rearrange("p (m t) -> p m t", m=HC)
        ps_k = bank[2][:, :].rearrange("p (m t) -> p m t", m=HC)
        ps_v = bank[3][:, :].rearrange("p (b d) -> p b d", b=NB)
        ps_s = bank[4][:, 0:NB * P].rearrange("p (b t) -> p b t", b=NB)
        ps_pt = bank[5][:, 0:NB * P].rearrange("p (b t) -> p b t", b=NB)
        ps_o = bank[6][:, :].rearrange("p (b d) -> p b d", b=NB)
        ps_f = bank[7]
        ps_st = bank[7][:, 0:4].rearrange("p (s c) -> p s c", s=2)
        ps_bt = bank[0][:, 0:HC * P].rearrange("p (c t) -> p c t", c=HC)
        ps_sim = [bank[1], bank[2]]
        ps_ln = [bank[3][:, 0:H], bank[6][:, 0:H]]
        ps_y = [bank[4][:, 0:H], bank[5][:, 0:H]]

        weights_in = sem("weights_in")
        fold_in = sem("fold_in")
        xa_in = [sem(f"xa_in{i}") for i in range(2)]
        xr_in = [sem(f"xr_in{i}") for i in range(2)]
        x2_out = [sem(f"x2_out{i}") for i in range(2)]
        ln2_out = [sem(f"ln2_out{i}") for i in range(2)]
        lnb_in = [sem(f"lnb_in{i}") for i in range(2)]
        xres_in = [sem(f"xres_in{i}") for i in range(2)]
        rows_in = [sem(f"rows_in{h}") for h in range(NH)]
        out_done = [sem(f"out_done{i}") for i in range(2)]
        const_step = sem("const_step")
        const_ready = sem("const_ready")
        mv_set = sem("mv_set")
        bn_seen = sem("bn_seen")
        mv_ready = sem("mv_ready")
        veps_ready = sem("veps_ready")
        lnv_ready = sem("lnv_ready")
        seed_ready = sem("seed_ready")
        newton = sem("newton")
        rcp_ready = sem("rcp_ready")
        x2_ready = sem("x2_ready")
        ln_ready = sem("ln_ready")
        ln2_ready = sem("ln2_ready")
        v_ready = sem("v_ready")
        masked = sem("masked")
        nmax_ready = sem("nmax_ready")
        q_ready = sem("q_ready")
        k_ready = sem("k_ready")
        prT_ready = sem("prT_ready")
        lnT_ready = sem("lnT_ready")
        p_ready = sem("p_ready")
        t_done = sem("t_done")
        q_done = sem("q_done")
        k_done = sem("k_done")
        v_done = sem("v_done")
        pt_done = sem("pt_done")
        s_done = sem("s_done")
        o_done = sem("o_done")
        sq_ready = sem("sq_ready")
        stats_added = sem("stats_added")
        fold_done = sem("fold_done")
        fold_copied = sem("fold_copied")
        stat_done = sem("stat_done")
        bs_step = sem("bs_step")
        bs_veps = sem("bs_veps")
        bs_lnv = sem("bs_lnv")
        bs_seed = sem("bs_seed")
        shift_ready = sem("shift_ready")
        fold_n_ready = sem("fold_n_ready")
        shift_done = sem("shift_done")
        fold_b_ready = sem("fold_b_ready")
        bt_done = sem("bt_done")
        lnbT_ready = sem("lnbT_ready")
        psln_ready = sem("psln_ready")
        sim_done = sem("sim_done")
        top_ready = sem("top_ready")
        topi_ready = sem("topi_ready")
        pair_ready = sem("pair_ready")
        best_ready = sem("best_ready")
        besti_ready = sem("besti_ready")
        pos_ready = sem("pos_ready")
        hot_ready = sem("hot_ready")
        hotv_ready = sem("hotv_ready")
        part_ready = sem("part_ready")
        idx_ready = sem("idx_ready")
        tanh_ready = sem("tanh_ready")
        hid_ready = sem("hid_ready")
        gel_ready = sem("gel_ready")
        coef_ready = sem("coef_ready")
        diag_ready = sem("diag_ready")
        rows_used = sem("rows_used")
        outb_ready = sem("outb_ready")

        block = ctx.enter_context(nc.Block())

        def known(i):
            return isinstance(i, int)

        def is_step(i):
            return not known(i) or 0 <= i < STEPS

        def is_tile(t):
            return not known(t) or 0 <= t < TILES

        def wait(eng, s, value):
            if not known(value) or value > 0:
                eng.wait_ge(s, value)

        def wait_apart(eng, s, value):
            if not known(value) or value > 0:
                eng.wait_ge(s, value)
                eng.nop(nofuse=True)

        def rounds(eng, first, last, body, regular_from, regular_to):
            for i in range(first, regular_from):
                body(i // 2, i % 2)
            with eng.Fori(regular_from // 2, (regular_to + 1) // 2) as half:
                body(half, 0)
                body(half, 1)
            for i in range(regular_to + 1, last + 1):
                body(i // 2, i % 2)

        A_FROM, A_TO = 4, 29
        B_FROM, B_TO = 4, 61

        @block.sync
        def _(sp):
            for dst, src in ((wq_sb, wq), (wk_sb, wk), (wv_sb, wv)):
                sp.dma_start(dst[:, :, :], src.rearrange("(c p) n -> p c n", p=P)).then_inc(weights_in, 16)
            sp.dma_start(bv_sb[:, :], bv.rearrange("(a n) -> a n", a=1).broadcast_to([P, H])).then_inc(weights_in, 16)
            for dst, src in ((bq_sb, bq), (bk_sb, bk), (gamma_sb, gamma), (beta_sb, beta)):
                sp.dma_start(dst[:, :], src.rearrange("(c p) -> p c", p=P),
                             allow_slow_non_contiguous=True).then_inc(weights_in, 16)

            def attention(half, par):
                i = 2 * half + par
                if is_step(i + 2):
                    wait(sp, ln_ready, i + 1)
                    sp.dma_start(xa[par], x_s[bass.ds(QS * (i + 2), P), :, :]).then_inc(xa_in[par], 16)
                if is_step(i - 1):
                    wait(sp, x2_ready, i - 2)
                    sp.dma_start(xr[1 - par], x_s[bass.ds(QS * (i - 1), P), :, :]).then_inc(xr_in[1 - par], 16)
                if is_step(i - 2):
                    n = i - 2
                    lo = 0 if known(n) and n == 0 else W
                    hi = P if known(n) and n == STEPS - 1 else P - W
                    wait(sp, x2_ready, n + 1)
                    sp.dma_start(x2_s[bass.ds(QS * n + lo, hi - lo), :, :], x2[par][lo:hi]).then_inc(x2_out[par], 16)
                    wait(sp, ln2_ready, n + 1)
                    sp.dma_start(ln2_s[bass.ds(QS * n + lo, hi - lo), :, :], ln2[par][lo:hi]).then_inc(ln2_out[par], 16)

            for i in (-2, -1):
                attention(i // 2, i % 2)
                if i == -2:
                    sp.dma_start(wquery_sb, w_query.rearrange("(u p) n -> p u n", p=P)).then_inc(fold_in, 16)
                    sp.dma_start(keys_sb, keys_t).then_inc(fold_in, 16)
            rounds(sp, 0, STEPS + 1, attention, A_FROM, A_TO)
            for par in range(2):
                n = (STEPS + 1 - par) // 2
                sp.wait_ge(x2_out[par], 16 * n)
                sp.wait_ge(ln2_out[par], 16 * n)

            def experts(half, par):
                t = 2 * half + par
                if is_tile(t + 1):
                    wait(sp, bt_done, t)
                    wait(sp, psln_ready, t)
                    sp.dma_start(lnb[1 - par][:, :], ln2_t[bass.ds(P * (t + 1), P), :]).then_inc(lnb_in[1 - par], 16)
                if is_tile(t):
                    wait(sp, outb_ready, t - 1)
                    sp.dma_start(xres[par][:, :], x2_t[bass.ds(P * t, P), :]).then_inc(xres_in[par], 16)
                if is_tile(t - 1):
                    wait(sp, outb_ready, t)
                    sp.dma_start(out_t[bass.ds(P * (t - 1), P), :], outb[1 - par][:, :]).then_inc(out_done[1 - par], 16)

            rounds(sp, -1, TILES, experts, B_FROM, B_TO)
            for par in range(2):
                sp.wait_ge(out_done[par], 16 * TILES // 2)

        @block.gpsimd
        def _(pool):
            g = nc.gpsimd
            g.memset(ident[:, :], 0.0).then_inc(const_step, 1)
            g.memset(half_ident[:, :], 0.0).then_inc(const_step, 1)
            g.memset(band[:, :], 0.0).then_inc(const_step, 1)
            g.memset(valid[:, :], 1.0).then_inc(const_step, 1)
            g.memset(ones_row[:, :], 1.0).then_inc(const_step, 1)
            g.iota(iota8[:, :], [[1, K]], base=0, channel_multiplier=0,
                   allow_small_or_imprecise_dtypes=True).then_inc(const_step, 1)
            pool.wait_ge(const_step, 6)
            g.affine_select(out=ident[:, :], in_=ident[:, :], compare_op=ALU.not_equal, fill=1.0,
                            base=0, pattern=[[-1, P]], channel_multiplier=1).then_inc(const_step, 1)
            g.affine_select(out=band[:, :], in_=band[:, :], compare_op=ALU.is_ge, fill=FAR,
                            base=W, pattern=[[-1, P]], channel_multiplier=1).then_inc(const_step, 1)
            g.affine_select(out=valid[:, 0:2], in_=valid[:, 0:2], compare_op=ALU.is_ge, fill=0.0,
                            base=P - W - 1, pattern=[[0, 2]], channel_multiplier=-1).then_inc(const_step, 1)
            pool.wait_ge(const_step, 9)
            g.affine_select(out=band[:, :], in_=band[:, :], compare_op=ALU.is_ge, fill=FAR,
                            base=W, pattern=[[1, P]], channel_multiplier=-1).then_inc(const_step, 1)
            g.affine_select(out=valid[:, 1:3], in_=valid[:, 1:3], compare_op=ALU.is_ge, fill=0.0,
                            base=-W, pattern=[[0, 2]], channel_multiplier=1).then_inc(const_step, 1)
            g.affine_select(out=half_ident[:, :], in_=half_ident[:, :], compare_op=ALU.not_equal, fill=0.5,
                            base=0, pattern=[[-1, P]], channel_multiplier=1).then_inc(const_step, 1)
            pool.wait_ge(const_step, 12)
            g.memset(rcp[:, :], 1.0).then_inc(const_ready, 1)

            def batch_sums(half, par):
                n = 2 * half + par
                kind = 0 if known(n) and n == 0 else 2 if known(n) and n == STEPS - 1 else 1
                first = kind != 1 or (known(n) and n == 1)
                l2 = ln2[par].rearrange("p b d -> p (b d)")
                wait(pool, ln2_ready, n + 1)
                if first:
                    g.tensor_copy(acc[:, kind, 0, :], l2).then_inc(stats_added, 1)
                    g.tensor_tensor(acc[:, kind, 1, :], l2, l2, ALU.mult).then_inc(stats_added, 1)
                else:
                    wait(pool, stats_added, 2 * n)
                    g.tensor_tensor(sq.rearrange("p b d -> p (b d)"), l2, l2, ALU.mult).then_inc(sq_ready, 1)
                    g.tensor_tensor(acc[:, kind, 0, :], acc[:, kind, 0, :], l2, ALU.add).then_inc(stats_added, 1)
                    wait(pool, sq_ready, n - 1)
                    g.tensor_tensor(acc[:, kind, 1, :], acc[:, kind, 1, :],
                                    sq.rearrange("p b d -> p (b d)"), ALU.add).then_inc(stats_added, 1)

            rounds(pool, 0, STEPS - 1, batch_sums, 4, 31)

            def gather(half, par):
                t = 2 * half + par
                wait_apart(pool, idx_ready, t + 1)
                for h in range(NH):
                    wait_apart(pool, rows_used, NH * (t - 1) + h + 1)
                    for k in range(K):
                        g.indirect_dma_start(
                            out=rows[:, h, k, :], out_offset=None, in_=table,
                            in_offset=bass.IndirectOffsetOnAxis(ap=idx[par][:, K * h + k:K * h + k + 1], axis=0),
                        ).then_inc(rows_in[h], 16)

            rounds(pool, 0, TILES - 1, gather, 4, 63)

        @block.tensor
        def _(pe):
            mm = nc.tensor.matmul
            pe.wait_ge(const_ready, 1)
            pe.wait_ge(fold_in, 32)
            for n in range(4):
                c, u0 = n // 2, NH * (n % 2)
                pe.wait_ge(fold_copied, n) if n else None
                for u in range(u0, u0 + NH):
                    last = mm(ps_f[:, (u - u0) * NK:(u - u0 + 1) * NK], wquery_sb[:, u, c * P:(c + 1) * P],
                              keys_sb[:, u, :], start=True, stop=True)
                last.then_inc(fold_done, 1)
            pe.wait_ge(weights_in, 16 * 8)

            def transposes(n):
                wait(pe, ln_ready, n + 1)
                for c in range(HC):
                    for b in range(NB):
                        last = nc.tensor.transpose(ps_t[:, c, b, :], ln[:, b, c * P:(c + 1) * P], ident[:, :])
                last.then_inc(t_done, 1)

            def attention(half, par):
                i = 2 * half + par
                if is_step(i):
                    wait(pe, lnT_ready, i + 1)
                    for ps, w, freed, done in ((ps_q, wq_sb, q_ready, q_done), (ps_k, wk_sb, k_ready, k_done)):
                        wait(pe, freed, i)
                        for m in range(HC):
                            for c in range(HC):
                                last = mm(ps[:, m, :], w[:, c, m * P:(m + 1) * P],
                                          lnT[:, c, :, :].rearrange("p b t -> p (b t)"),
                                          start=(c == 0), stop=(c == HC - 1))
                        last.then_inc(done, 1)
                    wait(pe, v_ready, i)
                    for b in range(NB):
                        for c in range(HC):
                            last = mm(ps_v[:, b, :], lnT[:, c, b, :], wv_sb[:, c, :], start=(c == 0), stop=(c == HC - 1))
                    last.then_inc(v_done, 1)
                if is_step(i - 1):
                    wait(pe, prT_ready, i - 1)
                    wait(pe, p_ready, i)
                    for b in range(NB):
                        last = nc.tensor.transpose(ps_pt[:, b, :], pr[:, b, :], ident[:, :])
                    last.then_inc(pt_done, 1)
                if is_step(i + 1):
                    transposes(i + 1)
                if is_step(i):
                    wait(pe, q_ready, i + 1)
                    wait(pe, k_ready, i + 1)
                    for b in range(NB):
                        for c in range(HC):
                            last = mm(ps_s[:, b, :], qT[:, c, b * P:(b + 1) * P], kT[:, c, b * P:(b + 1) * P],
                                      start=(c == 0), stop=(c == HC - 1))
                    last.then_inc(s_done, 1)
                if is_step(i - 1):
                    wait(pe, prT_ready, i)
                    wait(pe, v_ready, i)
                    wait(pe, x2_ready, i - 1)
                    for b in range(NB):
                        last = mm(ps_o[:, b, :], prT[:, b, :], v_sb[1 - par][:, b, :], start=True, stop=True)
                    last.then_inc(o_done, 1)

            rounds(pe, -1, STEPS, attention, 4, 31)

            pe.wait_ge(stats_added, 2 * STEPS)
            pe.wait_ge(fold_copied, 4)
            for s in range(2):
                for c in range(HC):
                    parts = [(kind, b) for kind in range(3) for b in range(NB)]
                    for n, (kind, b) in enumerate(parts):
                        lo = b * H + c * P
                        last = mm(ps_st[:, s, c:c + 1], acc[:, kind, s, lo:lo + P], valid[:, kind:kind + 1],
                                  start=(n == 0), stop=(n == len(parts) - 1))
            last.then_inc(stat_done, 1)
            pe.wait_ge(shift_ready, 1)
            for n in range(2):
                for c in range(HC):
                    last = mm(ps_sim[n][0:1, :], bs[:, 10, c:c + 1], fold[:, c, n * 512:(n + 1) * 512],
                              start=(c == 0), stop=(c == HC - 1))
            last.then_inc(shift_done, 1)
            pe.wait_ge(fold_b_ready, 1)
            pe.wait_ge(fold_n_ready, 1)

            def add_experts(t, par, h):
                wait(pe, diag_ready, NH * t + h + 1)
                for k in range(K):
                    last = mm(ps_y[par], diag[h % 2][:, k, :], rows[:, h, k, H:2 * H],
                              start=(h == 0 and k == 0), stop=(h == NH - 1 and k == K - 1))
                last.then_inc(rows_used, 1)

            def experts(half, par):
                t = 2 * half + par
                if is_tile(t + 1):
                    wait(pe, lnbT_ready, t + 1)
                    wait(pe, lnb_in[1 - par], 16 * (half + 1 + par))
                    for c in range(HC):
                        last = nc.tensor.transpose(ps_bt[:, c, :], lnb[1 - par][:, c * P:(c + 1) * P], ident[:, :])
                    last.then_inc(bt_done, 1)
                if is_tile(t - 1):
                    add_experts(t - 1, 1 - par, NH - 1)
                if is_tile(t + 1):
                    wait(pe, lnbT_ready, t + 2)
                    wait(pe, topi_ready, UNITS * (t + 1))
                    for n in range(2):
                        cols = slice(n * 512, (n + 1) * 512)
                        for c in range(HC):
                            mm(ps_sim[n][:, :], lnbT[:, c, :], fold_n[:, c, cols], start=(c == 0), stop=False)
                        last = mm(ps_sim[n][:, :], ones_row[:, :], fold_b[:, cols], start=False, stop=True)
                    last.then_inc(sim_done, 1)
                if is_tile(t):
                    wait(pe, outb_ready, t - 1)
                    for h in range(NH - 1):
                        add_experts(t, par, h)

            rounds(pe, -1, TILES, experts, B_FROM, B_TO)

        @block.scalar
        def _(act):
            a = nc.scalar.activation
            act.wait_ge(weights_in, 16 * 8)
            for n in range(4):
                c, u0 = n // 2, NH * (n % 2)
                act.wait_ge(fold_done, n + 1)
                a(fold[:, c, u0 * NK:(u0 + NH) * NK], ps_f[:, :], ACT.Copy).then_inc(fold_copied, 1)

            def attention(half, par):
                i = 2 * half + par
                if is_step(i):
                    wait(act, q_done, i + 1)
                    for m in range(HC):
                        last = a(qT[:, m, :], ps_q[:, m, :], ACT.Identity, bias=bq_sb[:, m:m + 1])
                    last.then_inc(q_ready, 1)
                wait(act, veps_ready, i + 2)
                a(lnv[:, :], veps[:, :], ACT.Ln).then_inc(lnv_ready, 1)
                wait(act, lnv_ready, i + 2)
                a(y0[:, :], lnv[:, :], ACT.Exp, scale=-0.5).then_inc(seed_ready, 1)
                if is_step(i):
                    wait(act, k_done, i + 1)
                    for m in range(HC):
                        last = a(kT[:, m, :], ps_k[:, m, :], ACT.Identity, bias=bk_sb[:, m:m + 1])
                    last.then_inc(k_ready, 1)
                if is_step(i - 1):
                    wait(act, pt_done, i)
                    a(prT, ps_pt, ACT.Copy).then_inc(prT_ready, 1)
                if is_step(i + 1):
                    wait(act, t_done, i + 2)
                    a(lnT, ps_t, ACT.Copy).then_inc(lnT_ready, 1)
                if is_step(i):
                    wait(act, nmax_ready, i + 1)
                    for b in range(NB):
                        last = a(pr[:, b, :], sm[:, b, :], ACT.Exp, bias=nmax[:, b:b + 1],
                                 accum_out=rsum[par][:, b:b + 1])
                    last.then_inc(p_ready, 1)

            rounds(act, -1, STEPS + 1, attention, 4, 31)

            act.wait_ge(bs_veps, 1)
            a(bs[:, 4, :], bs[:, 3, :], ACT.Ln).then_inc(bs_lnv, 1)
            act.wait_ge(bs_lnv, 1)
            a(bs[:, 5, :], bs[:, 4, :], ACT.Exp, scale=-0.5).then_inc(bs_seed, 1)
            act.wait_ge(shift_done, 1)
            for n in range(2):
                last = a(fold_b[:, n * 512:(n + 1) * 512], ps_sim[n][0:1, :], ACT.Copy)
            last.then_inc(fold_b_ready, 1)

            def spread(t, par, h):
                wait(act, rows_used, NH * t + h - 1)
                wait(act, coef_ready, NH * t + h + 1)
                for k in range(K):
                    last = a(diag[h % 2][:, k, :], half_ident[:, :], ACT.Copy, scale=coef[par][:, K * h + k:K * h + k + 1])
                last.then_inc(diag_ready, 1)

            def experts(half, par):
                t = 2 * half + par
                if is_tile(t + 1):
                    wait(act, bt_done, t + 2)
                    a(lnbT[:, :, :], ps_bt, ACT.Copy).then_inc(lnbT_ready, 1)
                    wait(act, hid_ready, NH * t)
                    wait(act, lnb_in[1 - par], 16 * (half + 1 + par))
                    a(ps_ln[1 - par], lnb[1 - par][:, :], ACT.Copy).then_inc(psln_ready, 1)
                if is_tile(t - 1):
                    spread(t - 1, 1 - par, NH - 1)
                if is_tile(t):
                    for h in range(NH):
                        wait(act, hid_ready, NH * t + h + 1)
                        cols = slice(K * h, K * (h + 1))
                        a(gel[par][:, cols], hid[par][:, cols], ACT.Gelu).then_inc(gel_ready, 1)
                        if h:
                            spread(t, par, h - 1)
                        if h == 4 and is_tile(t + 1):
                            wait(act, best_ready, NH * (t + 2))
                            a(tanh[1 - par][:, :], best[:, :, :].rearrange("p h k -> p (h k)"),
                              ACT.Tanh, scale=0.5).then_inc(tanh_ready, 1)
                elif is_tile(t + 1):
                    wait(act, best_ready, NH * (t + 2))
                    a(tanh[1 - par][:, :], best[:, :, :].rearrange("p h k -> p (h k)"),
                      ACT.Tanh, scale=0.5).then_inc(tanh_ready, 1)

            rounds(act, -1, TILES, experts, B_FROM, B_TO)

        @block.vector
        def _(dve):
            v = nc.vector
            v.memset(mv[:, :, :], 1.0).then_inc(mv_set, 1)
            dve.wait_ge(mv_set, 1)
            dve.wait_ge(const_ready, 1)
            dve.wait_ge(weights_in, 16 * 8)

            def refine(var, y, a1, a2, a3, res, count, base):
                v.tensor_tensor(a1, y, y, ALU.mult).then_inc(count, 1)
                wait(dve, count, base + 1)
                v.tensor_tensor(a2, a1, var, ALU.mult).then_inc(count, 1)
                wait(dve, count, base + 2)
                v.tensor_scalar(a3, a2, -0.5, 1.5, ALU.mult, ALU.add).then_inc(count, 1)
                wait(dve, count, base + 3)
                v.tensor_tensor(res, y, a3, ALU.mult).then_inc(count, 1)
                wait_apart(dve, count, base + 4)

            def attention(half, par):
                i = 2 * half + par
                ahead, behind = is_step(i + 1), is_step(i - 2)
                if behind:
                    n = i - 2
                    wait(dve, p_ready, n + 1)
                    v.reciprocal(rcp[:, :], rsum[par][:, :]).then_inc(rcp_ready, 1)
                if ahead:
                    wait(dve, xa_in[1 - par], 16 * (half + 1 + par))
                    for b in range(NB):
                        last = v.bn_stats(bst[:, b, :], xa[1 - par][:, b, :])
                if behind:
                    wait(dve, rcp_ready, n + 1)
                    wait(dve, o_done, n + 1)
                    wait(dve, xr_in[par], 16 * half)
                    wait(dve, x2_out[par], 16 * (half - 1))
                    for b in range(NB):
                        last = v.scalar_tensor_tensor(x2[par][:, b, :], ps_o[:, b, :], rcp[:, b:b + 1],
                                                      xr[par][:, b, :], ALU.mult, ALU.add)
                    last.then_inc(x2_ready, 1)
                    wait(dve, x2_ready, n + 1)
                    for b in range(NB):
                        last = v.bn_stats(bst[:, NB + b, :], x2[par][:, b, :])
                lo, hi = 0 if ahead else NB, 2 * NB if behind else NB
                if ahead or behind:
                    last.then_inc(bn_seen, 1)
                    wait_apart(dve, bn_seen, i + 2)
                    for b in range(lo, hi):
                        last = v.bn_aggr(mv[:, b, :], bst[:, b, :])
                    last.then_inc(mv_ready, 1)
                else:
                    v.memset(y2[:, :], 1.0).then_inc(bn_seen, 1)
                    v.memset(y3[:, :], 1.0).then_inc(mv_ready, 1)
                wait(dve, mv_ready, i + 2)
                v.tensor_scalar(veps[:, :], mv[:, :, 1], EPS, None, ALU.add).then_inc(veps_ready, 1)
                if is_step(i):
                    wait(dve, v_done, i + 1)
                    wait(dve, o_done, i - 1)
                    v.tensor_tensor(v_sb[par], ps_v, bv_sb[:, :].unsqueeze(1).broadcast_to([P, NB, H]),
                                    ALU.add).then_inc(v_ready, 1)
                wait(dve, seed_ready, i + 2)
                refine(veps[:, :], y0[:, :], y2[:, :], y3[:, :], y4[:, :], rstd[:, :], newton, 4 * (i + 1))
                if ahead:
                    wait(dve, t_done, i + 1)
                    for b in range(NB):
                        last = v.tensor_scalar(ln[:, b, :], xa[1 - par][:, b, :], mv[:, b, 0:1], rstd[:, b:b + 1],
                                               ALU.subtract, ALU.mult)
                    last.then_inc(ln_ready, 1)
                if behind:
                    wait(dve, ln2_out[par], 16 * (half - 1))
                    wait(dve, stats_added, 2 * (n - 1))
                    for b in range(NB):
                        last = v.tensor_scalar(ln2[par][:, b, :], x2[par][:, b, :], mv[:, NB + b, 0:1],
                                               rstd[:, NB + b:NB + b + 1], ALU.subtract, ALU.mult)
                    last.then_inc(ln2_ready, 1)
                if is_step(i):
                    wait(dve, s_done, i + 1)
                    v.scalar_tensor_tensor(sm, ps_s, SCALE, band[:, :].unsqueeze(1).broadcast_to([P, NB, P]),
                                           ALU.mult, ALU.add).then_inc(masked, 1)
                    wait(dve, masked, i + 1)
                    v.tensor_reduce(nmax[:, :], sm, AX.X, ALU.max, negate=True).then_inc(nmax_ready, 1)

            rounds(dve, -1, STEPS + 1, attention, 4, 31)

            count = [0]

            def then(ins):
                count[0] += 1
                ins.then_inc(bs_step, 1)
                dve.wait_ge(bs_step, count[0])

            dve.wait_ge(stat_done, 1)
            mean, ex2, msq, var_e, _, seed, a1, a2, a3, inv, shift, fac = (bs[:, n, :] for n in range(12))
            then(v.tensor_scalar(mean, ps_st[:, 0, :], 1.0 / TOKENS, None, ALU.mult))
            then(v.tensor_scalar(ex2, ps_st[:, 1, :], 1.0 / TOKENS, EPS, ALU.mult, ALU.add))
            then(v.tensor_tensor(msq, mean, mean, ALU.mult))
            v.tensor_tensor(var_e, ex2, msq, ALU.subtract).then_inc(bs_veps, 1)
            dve.wait_ge(bs_seed, 1)
            then(v.tensor_tensor(a1, seed, seed, ALU.mult))
            then(v.tensor_tensor(a2, a1, var_e, ALU.mult))
            then(v.tensor_scalar(a3, a2, -0.5, 1.5, ALU.mult, ALU.add))
            then(v.tensor_tensor(inv, seed, a3, ALU.mult))
            then(v.tensor_tensor(fac, inv, gamma_sb[:, :], ALU.mult))
            then(v.tensor_tensor(a1, mean, fac, ALU.mult))
            v.tensor_tensor(shift, beta_sb[:, :], a1, ALU.subtract).then_inc(shift_ready, 1)
            for c in range(HC):
                last = v.tensor_scalar(fold_n[:, c, :], fold[:, c, :], fac[:, c:c + 1], None, ALU.mult)
            last.then_inc(fold_n_ready, 1)

            def dots(t, half, par, h):
                if h == 0:
                    wait(dve, psln_ready, t + 1)
                wait(dve, rows_in[h], 16 * K * (t + 1))
                for k in range(K):
                    last = v.tensor_tensor_reduce(
                        out=rows[:, h, k, 0:H], in0=rows[:, h, k, 0:H], in1=ps_ln[par], scale=1.0, scalar=0.0,
                        op0=ALU.mult, op1=ALU.add, accum_out=hid[par][:, K * h + k:K * h + k + 1])
                last.then_inc(hid_ready, 1)

            def gate(t, par, h):
                cols = slice(K * h, K * (h + 1))
                n = NH * t + h + 1
                wait(dve, gel_ready, n)
                if h == 0:
                    wait(dve, tanh_ready, t + 1)
                v.scalar_tensor_tensor(coef[par][:, cols], tanh[par][:, cols], 1.0, gel[par][:, cols],
                                       ALU.add, ALU.mult).then_inc(coef_ready, 1)

            def best_keys(n, p):
                if p == 0:
                    wait_apart(dve, sim_done, n + 1)
                for u in range(p * NH, (p + 1) * NH):
                    v.max(top[:, u, :], ps_sim[p][:, (u - p * NH) * NK:(u - p * NH + 1) * NK]).then_inc(top_ready, 1)
                wait_apart(dve, top_ready, UNITS * n + (p + 1) * NH)
                for u in range(p * NH, (p + 1) * NH):
                    v.max_index(topi[:, u, :], top[:, u, :],
                                ps_sim[p][:, (u - p * NH) * NK:(u - p * NH + 1) * NK]).then_inc(topi_ready, 1)
                if p == 1:
                    first = top[:, 0:NH, :].unsqueeze(3).broadcast_to([P, NH, K, K])
                    second = top[:, NH:UNITS, :].unsqueeze(2).broadcast_to([P, NH, K, K])
                    v.tensor_tensor(pair[:, :, :].rearrange("p h (i j) -> p h i j", i=K), first, second,
                                    ALU.add).then_inc(pair_ready, 1)

            def best_pairs(n):
                wait(dve, tanh_ready, n)
                wait_apart(dve, pair_ready, n + 1)
                for h in range(NH):
                    v.max(best[:, h, :], pair[:, h, :]).then_inc(best_ready, 1)
                wait_apart(dve, best_ready, NH * (n + 1))
                for h in range(NH):
                    last = v.max_index(besti[:, K * h:K * (h + 1)], best[:, h, :], pair[:, h, :])
                last.then_inc(besti_ready, 1)

            def name_rows(n, par):
                wait(dve, besti_ready, n + 1)
                v.tensor_scalar(pos[:, 0, :], besti[:, :], 3, None, ALU.logical_shift_right).then_inc(pos_ready, 1)
                v.tensor_scalar(pos[:, 1, :], besti[:, :], K - 1, None, ALU.bitwise_and).then_inc(pos_ready, 1)
                wait(dve, pos_ready, 2 * (n + 1))
                v.tensor_tensor(hot[:, :, :, :].rearrange("p s n k -> p (s n) k"),
                                pos[:, :, :].rearrange("p s n -> p (s n)").unsqueeze(2).broadcast_to([P, 2 * NH * K, K]),
                                iota8[:, :].unsqueeze(1).broadcast_to([P, 2 * NH * K, K]),
                                ALU.is_equal).then_inc(hot_ready, 1)
                wait(dve, hot_ready, n + 1)
                wait(dve, topi_ready, UNITS * (n + 1))
                for s in range(2):
                    v.tensor_tensor(hotv[:, s, :, :].rearrange("p (h k) m -> p h k m", h=NH),
                                    hot[:, s, :, :].rearrange("p (h k) m -> p h k m", h=NH),
                                    topi[:, s * NH:(s + 1) * NH, :].unsqueeze(2).broadcast_to([P, NH, K, K]),
                                    ALU.mult).then_inc(hotv_ready, 1)
                wait(dve, hotv_ready, 2 * (n + 1))
                v.tensor_reduce(part[:, :, :], hotv[:, :, :, :], AX.X, ALU.add).then_inc(part_ready, 1)
                wait(dve, part_ready, n + 1)
                v.scalar_tensor_tensor(idx[par][:, :], part[:, 0, :], float(NK), part[:, 1, :],
                                       ALU.mult, ALU.add).then_inc(idx_ready, 1)

            def finish(t, half, par):
                wait(dve, rows_used, NH * (t + 1))
                wait(dve, xres_in[par], 16 * (half + 1))
                wait(dve, out_done[par], 16 * half)
                v.tensor_tensor(outb[par][:, :], ps_y[par], xres[par][:, :], ALU.add).then_inc(outb_ready, 1)

            def experts(half, par):
                t = 2 * half + par
                for h in range(NH):
                    if is_tile(t):
                        dots(t, half, par, h)
                    if h == 0 and is_tile(t - 1):
                        gate(t - 1, 1 - par, NH - 1)
                    if h > 0 and is_tile(t):
                        gate(t, par, h - 1)
                    if is_tile(t + 1):
                        if h in (0, 1):
                            best_keys(t + 1, h)
                        if h == 2:
                            best_pairs(t + 1)
                        if h == 3:
                            name_rows(t + 1, 1 - par)
                    if h == 4 and is_tile(t - 1):
                        finish(t - 1, half if par else half - 1, 1 - par)

            rounds(dve, -1, TILES, experts, B_FROM, B_TO)


def kernel(L0_attn_sequence_output, L0_attn_Wq, L0_attn_bq, L0_attn_Wk, L0_attn_bk, L0_attn_Wv, L0_attn_bv,
           L0_ffn_bn_gamma, L0_ffn_bn_beta, L0_ffn_w_q, L0_ffn_keys_p, L0_ffn_down, L0_ffn_up):
    import numpy as np
    import concourse.bacc as bacc
    from concourse.bass_utils import run_bass_kernel_spmd

    keys = np.asarray(L0_ffn_keys_p)
    nh, nk, halves, kd = keys.shape
    arrays = {
        "x": L0_attn_sequence_output, "wq": L0_attn_Wq, "bq": L0_attn_bq, "wk": L0_attn_Wk, "bk": L0_attn_bk,
        "wv": L0_attn_Wv, "bv": L0_attn_bv, "gamma": L0_ffn_bn_gamma, "beta": L0_ffn_bn_beta,
        "w_query": L0_ffn_w_q,
        "keys_t": keys.transpose(3, 2, 0, 1).reshape(kd, halves * nh, nk),
        "table": np.concatenate([np.asarray(L0_ffn_down), np.asarray(L0_ffn_up)], axis=1),
    }
    arrays = {n: np.ascontiguousarray(a) for n, a in arrays.items()}
    nc = bacc.Bacc("TRN2", target_bir_lowering=False, num_devices=1)
    args = [nc.dram_tensor(n, a.shape, mybir.dt.from_np(a.dtype), kind="ExternalInput").ap()
            for n, a in arrays.items()]
    shape = arrays["x"].shape
    out = nc.dram_tensor("out", shape, mybir.dt.float32, kind="ExternalOutput").ap()
    window_attention_peer_kernel(nc, *args, out)
    r = run_bass_kernel_spmd(nc, [arrays], core_ids=[0])
    return r.results[0]["out"]
```

```python
import concourse.bass as bass
from concourse import mybir
from contextlib import ExitStack



def window_attention_peer_kernel(
    nc: bass.Bass,
    x: bass.AP,
    wq_t: bass.AP,
    bq: bass.AP,
    wk_t: bass.AP,
    bk: bass.AP,
    wv: bass.AP,
    bv: bass.AP,
    gamma: bass.AP,
    beta: bass.AP,
    w_query: bass.AP,
    keys_t: bass.AP,
    down_t: bass.AP,
    up_c: bass.AP,
    out: bass.AP,
):
    f32 = mybir.dt.float32
    u32 = mybir.dt.uint32
    ALU = mybir.AluOpType
    ACT = mybir.ActivationFunctionType
    AX = mybir.AxisListType

    P = 128
    NB, S, H = x.shape
    HC = H // P
    W = 2
    QS = P - 2 * W
    STEPS = (S - P) // QS + 1
    assert (STEPS - 1) * QS + P == S
    SCALE = float(H) ** -0.5
    EPS = 1e-5
    FAR = -1.0e30
    NH = 8
    K = 8
    NK = keys_t.shape[2]
    UNITS = 2 * NH
    TOKENS = NB * S
    TILES = TOKENS // P
    GT = 2 * P
    GROUPS = TOKENS // GT
    SEL = NH * K
    CH = NK * NK // P
    HK = NK // 2
    ST = 16
    CS, PS = CH // ST, P // ST
    TS = ST // 2

    ctx = ExitStack()
    with ctx:
        def sb(name, shape, dt=f32):
            return ctx.enter_context(nc.sbuf_tensor(name, shape, dt))

        def sem(name):
            return ctx.enter_context(nc.semaphore(name))

        x_s = x.rearrange("b s d -> s b d")
        x2_d = nc.dram_tensor("x2_scratch", (NB, S, H), f32, kind="Internal").ap()
        ln2_d = nc.dram_tensor("ln2_scratch", (NB, S, H), f32, kind="Internal").ap()
        x2_s = x2_d.rearrange("b s d -> s b d")
        ln2_s = ln2_d.rearrange("b s d -> s b d")
        x2_t = x2_d.rearrange("b s d -> (b s) d")
        ln2_t = ln2_d.rearrange("b s d -> (b s) d")
        out_t = out.rearrange("b s d -> (b s) d")

        ident = sb("ident", [P, P])
        band = sb("band", [P, P])
        valid = sb("valid", [P, 3])
        iota8 = sb("iota8", [P, K])
        iota_rows = sb("iota_rows", [P, P])
        iota_cols = sb("iota_cols", [P, 2, HK])
        ones = sb("ones", [P, P])
        c_sb = sb("c_sb", [P, HC])
        bqk = sb("bqk", [P, HC])
        bqk_sb = sb("bqk_sb", [P, 1])
        bq_sb = sb("bq_sb", [P, HC])
        bk_sb = sb("bk_sb", [P, HC])
        gamma_sb = sb("gamma_sb", [P, HC])
        beta_sb = sb("beta_sb", [P, HC])
        fold = sb("fold", [P, HC, UNITS * NK])

        arena = sb("arena", [P, 4, CH * H])
        down = arena[:, 0, :].rearrange("p (k c e) -> p k c e", k=HC, c=CH)
        up = arena[:, 1, :].rearrange("p (c d) -> p c d", c=CH)
        gates = [arena[:, 2 + i, :].rearrange("p (c t) -> p c t", c=CH) for i in range(2)]
        wquery_sb = arena[:, 1, 0:UNITS * H].rearrange("p (u d) -> p u d", u=UNITS)
        keys_sb = arena[:, 1, UNITS * H:UNITS * (H + NK)].rearrange("p (u k) -> p u k", u=UNITS)
        flat = arena[:, 2:4, :].rearrange("p a b -> p (a b)")
        spot = [0]

        def shared(*dims):
            n = 1
            for d in dims:
                n *= d
            v = flat[:, spot[0]:spot[0] + n]
            spot[0] += n
            assert spot[0] <= 2 * CH * H
            names = "abcd"[:len(dims)]
            if len(dims) == 1:
                return v
            return v.rearrange(f"p ({' '.join(names)}) -> p {' '.join(names)}",
                               **{c: d for c, d in zip(names, dims)})

        a_sb = shared(HC, H)
        wvu_sb = shared(HC, H + 1)
        bv_sb = shared(H)
        wqT_sb = shared(HC, H)
        wkT_sb = shared(HC, H)
        xa = [shared(NB, H) for _ in range(2)]
        xr = [shared(NB, H) for _ in range(2)]
        ln = shared(NB, H)
        lnT = shared(HC, NB, P)
        gT = shared(HC, NB * P)
        vu = [shared(NB, H + 1) for _ in range(2)]
        sm = shared(NB, P)
        pr = shared(NB, P)
        prT = shared(NB, P)
        x2 = [shared(NB, H) for _ in range(2)]
        ln2 = [shared(NB, H) for _ in range(2)]
        sq = shared(NB, H)
        acc_mid = shared(2, NB * H)
        acc_edge = shared(3, 2, H)
        bst = sb("bst", [P, 4, 6])
        mv = sb("mv", [P, 4, 2])
        veps = sb("veps", [P, 4])
        rstd = sb("rstd", [P, 4])
        root_a = sb("root_a", [P, 4])
        root_b = sb("root_b", [P, 4])
        nmax = sb("nmax", [P, NB])
        rsum = [sb(f"rsum{i}", [P, NB]) for i in range(2)]
        rcp = sb("rcp", [P, NB])
        bs = sb("bs", [P, 9, HC])
        mean, ex2, msq, bvar, inv, bs_a, bs_b, factor, shift = (bs[:, n, :] for n in range(9))

        lnb = [sb(f"lnb{i}", [P, 2, H]) for i in range(2)]
        lnr = sb("lnr", [P, 2, H])
        lnbT = sb("lnbT", [P, HC, P])
        lnT2 = [sb(f"lnT2{i}", [P, HC, GT]) for i in range(2)]
        xres = [sb(f"xres{i}", [P, 2, H]) for i in range(2)]
        top = sb("top", [P, UNITS, K])
        topi = sb("topi", [P, UNITS, K], u32)
        pair = sb("pair", [P, NH, K * K])
        best = sb("best", [P, NH, K])
        besti = sb("besti", [P, SEL], u32)
        pos = sb("pos", [P, 2, SEL], u32)
        hot = sb("hot", [P, 2, SEL, K])
        part = sb("part", [P, 2, SEL])
        upper = sb("upper", [P, SEL])
        codes = sb("codes", [P, 3, 2, SEL])
        codesT = [sb(f"codesT{i}", [P, 3, P // 2]) for i in range(2)]
        rows_hot = [sb(f"rows_hot{i}", [P, PS, P]) for i in range(2)]
        cols_hot = [sb(f"cols_hot{i}", [P, PS, 2 * HK]) for i in range(2)]
        cols_gate = [sb(f"cols_gate{i}", [P, PS, 2 * HK]) for i in range(2)]
        gel = [sb(f"gel{i}", [P, CS, GT]) for i in range(2)]
        wgt = [sb(f"wgt{i}", [P, CS, GT]) for i in range(2)]

        bank = [ctx.enter_context(nc.psum_tensor(f"bank{i}", [P, 512], f32)) for i in range(8)]
        ps_t = bank[0][:, :].rearrange("p (c b t) -> p c b t", c=HC, b=NB)
        ps_g = bank[1][:, :].rearrange("p (m t) -> p m t", m=HC)
        ps_v = [bank[3][:, 0:H + 1], bank[2][:, 0:H + 1]]
        ps_s = bank[4][:, 0:NB * P].rearrange("p (b t) -> p b t", b=NB)
        ps_pt = bank[5][:, 0:NB * P].rearrange("p (b t) -> p b t", b=NB)
        ps_o = bank[6][:, :].rearrange("p (b d) -> p b d", b=NB)
        ps_w = bank[7][:, 0:HC * H].rearrange("p (c n) -> p c n", c=HC)
        ps_c = bank[1][:, 0:HC]
        ps_u = bank[3][:, 0:HC]
        ps_bqk = bank[2][:, 0:1]
        ps_fold = [bank[7], bank[7], bank[1], bank[3]]
        ps_stat = [[bank[2], bank[4]], [bank[5], bank[7]]]
        ps_bt = bank[0][:, 0:HC * P].rearrange("p (c t) -> p c t", c=HC)
        ps_ct = bank[0][:, 0:3 * P].rearrange("p (a t) -> p a t", a=3)
        ps_sim = [bank[1], bank[2]]
        ps_hid = [bank[3], bank[4]]
        ps_gate = [bank[5], bank[6]]
        ps_y = bank[7][:, :].rearrange("p (u d) -> p u d", u=2)

        weights_in = sem("weights_in")
        fold_in = sem("fold_in")
        xa_in = [sem(f"xa_in{i}") for i in range(2)]
        xr_in = [sem(f"xr_in{i}") for i in range(2)]
        x2_out = [sem(f"x2_out{i}") for i in range(2)]
        ln2_out = [sem(f"ln2_out{i}") for i in range(2)]
        lnb_in = [sem(f"lnb_in{i}") for i in range(2)]
        xres_in = [sem(f"xres_in{i}") for i in range(2)]
        lnr_in = sem("lnr_in")
        down_in = sem("down_in")
        up_in = sem("up_in")
        out_done = [sem(f"out_done{i}") for i in range(2)]
        const_step = sem("const_step")
        const_ready = sem("const_ready")
        mv_set = sem("mv_set")
        xa_seen = sem("xa_seen")
        x2_seen = sem("x2_seen")
        mv_ready = sem("mv_ready")
        veps_ready = sem("veps_ready")
        root_step = sem("root_step")
        xb_ready = sem("xb_ready")
        rcp_ready = sem("rcp_ready")
        x2_ready = sem("x2_ready")
        ln_ready = sem("ln_ready")
        ln2_ready = sem("ln2_ready")
        v_ready = sem("v_ready")
        masked = sem("masked")
        nmax_ready = sem("nmax_ready")
        g_ready = sem("g_ready")
        prT_ready = sem("prT_ready")
        lnT_ready = sem("lnT_ready")
        p_ready = sem("p_ready")
        t_done = sem("t_done")
        g_done = sem("g_done")
        v_done = sem("v_done")
        pt_done = sem("pt_done")
        s_done = sem("s_done")
        o_done = sem("o_done")
        sq_ready = sem("sq_ready")
        stats_added = sem("stats_added")
        weights_done = sem("weights_done")
        bqk_ready = sem("bqk_ready")
        bqk_scaled = sem("bqk_scaled")
        a_done = sem("a_done")
        a_ready = sem("a_ready")
        band_ready = sem("band_ready")
        fold_done = sem("fold_done")
        fold_copied = sem("fold_copied")
        last_step = sem("last_step")
        last_added = sem("last_added")
        stat_done = sem("stat_done")
        bs_step = sem("bs_step")
        norm_ready = sem("norm_ready")
        bt_done = sem("bt_done")
        bt_read = sem("bt_read")
        sim_done = sem("sim_done")
        top_ready = sem("top_ready")
        topi_ready = sem("topi_ready")
        pair_ready = sem("pair_ready")
        best_ready = sem("best_ready")
        besti_ready = sem("besti_ready")
        pos_ready = sem("pos_ready")
        hot_ready = sem("hot_ready")
        hotv_ready = sem("hotv_ready")
        part_ready = sem("part_ready")
        upper_ready = sem("upper_ready")
        codes_ready = sem("codes_ready")
        tanh_ready = sem("tanh_ready")
        ct_done = sem("ct_done")
        ct_read = sem("ct_read")
        rt_done = sem("rt_done")
        rt_read = sem("rt_read")
        hits_ready = sem("hits_ready")
        cols_ready = sem("cols_ready")
        gate_done = sem("gate_done")
        gate_read = sem("gate_read")
        hid_done = sem("hid_done")
        gel_ready = sem("gel_ready")
        wgt_ready = sem("wgt_ready")
        y_done = sem("y_done")
        y_added = sem("y_added")

        block = ctx.enter_context(nc.Block())

        def known(i):
            return isinstance(i, int)

        def is_step(i):
            return not known(i) or 0 <= i < STEPS

        def is_group(g):
            return not known(g) or 0 <= g < GROUPS

        def wait(eng, s, value):
            if not known(value) or value > 0:
                eng.wait_ge(s, value)

        def wait_apart(eng, s, value):
            if not known(value) or value > 0:
                eng.wait_ge(s, value)
                eng.nop(nofuse=True)

        def kept_rows(n):
            edge = known(n)
            return (0 if edge and n == 0 else W), (P if edge and n == STEPS - 1 else P - W)

        def rounds(eng, first, last, body, regular_from, regular_to):
            for i in range(first, regular_from):
                body(i // 2, i % 2)
            with eng.Fori(regular_from // 2, (regular_to + 1) // 2) as half:
                body(half, 0)
                body(half, 1)
            for i in range(regular_to + 1, last + 1):
                body(i // 2, i % 2)

        A_FROM, A_TO = 4, 29
        CODES_AT = (TS + 1, 1)
        INPUT_AT = (TS + 3, TS + 5)
        KEYS_AT, PAIRS_AT, NAMES_AT, TANH_AT = (2, 4), 5, 7, 6
        B_FROM, B_TO = 2, 27

        @block.sync
        def _(sp):
            def weights():
                for dst, src in ((wqT_sb, wq_t), (wkT_sb, wk_t), (wvu_sb[:, :, 0:H], wv)):
                    sp.dma_start(dst, src.rearrange("(c p) n -> p c n", p=P)).then_inc(weights_in, 16)
                for dst, src in ((bq_sb, bq), (bk_sb, bk), (gamma_sb, gamma), (beta_sb, beta)):
                    sp.dma_start(dst[:, :], src.rearrange("(c p) -> p c", p=P),
                                 allow_slow_non_contiguous=True).then_inc(weights_in, 16)
                sp.dma_start(bv_sb[:, :], bv.rearrange("(a n) -> a n", a=1).broadcast_to([P, H])).then_inc(weights_in, 16)

            def attention(half, par):
                i = 2 * half + par
                if is_step(i + 2):
                    wait(sp, ln_ready, i + 1)
                    sp.dma_start(xa[par], x_s[bass.ds(QS * (i + 2), P), :, :]).then_inc(xa_in[par], 16)
                if is_step(i - 4):
                    n = i - 4
                    lo, hi = kept_rows(n)
                    wait(sp, ln2_ready, n + 1)
                    sp.dma_start(ln2_s[bass.ds(QS * n + lo, hi - lo), :, :], ln2[par][lo:hi]).then_inc(ln2_out[par], 16)
                if is_step(i - 1):
                    wait(sp, x2_ready, i - 2)
                    sp.dma_start(xr[1 - par], x_s[bass.ds(QS * (i - 1), P), :, :]).then_inc(xr_in[1 - par], 16)
                if is_step(i - 2):
                    n = i - 2
                    lo, hi = kept_rows(n)
                    wait(sp, x2_ready, n + 1)
                    sp.dma_start(x2_s[bass.ds(QS * n + lo, hi - lo), :, :], x2[par][lo:hi]).then_inc(x2_out[par], 16)

            attention(-1, 0)
            weights()
            attention(-1, 1)
            sp.dma_start(wquery_sb, w_query.rearrange("(u p) n -> p u n", p=P)).then_inc(fold_in, 16)
            sp.dma_start(keys_sb, keys_t).then_inc(fold_in, 16)
            for i in range(2):
                attention(0, i)
            sp.dma_start(down, down_t.rearrange("(k p) (c e) -> p k c e", p=P, c=CH)).then_inc(down_in, 16)
            rounds(sp, 2, STEPS + 3, attention, 6, A_TO)

            def load_choices(g, par):
                wait(sp, bt_done, 2 * (g - 1))
                sp.dma_start(lnb[par][:, :, :], ln2_t[bass.ds(GT * g, GT), :].rearrange("(u p) d -> p u d", p=P)
                             ).then_inc(lnb_in[par], 16)

            sp.wait_ge(ln2_out[0], 32)
            sp.wait_ge(ln2_out[1], 16)
            load_choices(0, 0)
            sp.wait_ge(fold_done, 4)
            sp.dma_start(up, up_c.rearrange("(c p) d -> p c d", p=P)).then_inc(up_in, 16)
            for par in range(2):
                n = (STEPS + 1 - par) // 2
                sp.wait_ge(x2_out[par], 16 * n)
                sp.wait_ge(ln2_out[par], 16 * n)

            def experts(half, par):
                r = 2 * half + par
                if is_group(r + 3) and not (known(r) and r < -2):
                    load_choices(r + 3, 1 - par)
                if is_group(r + 2):
                    wait(sp, rt_done, 2 * (r + 2))
                    sp.dma_start(lnr[:, :, :], ln2_t[bass.ds(GT * (r + 2), GT), :].rearrange("(u p) d -> p u d", p=P)
                                 ).then_inc(lnr_in, 16)
                if is_group(r - 1):
                    wait(sp, y_added, r)
                    sp.dma_start(out_t[bass.ds(GT * (r - 1), GT), :].rearrange("(u p) d -> p u d", p=P),
                                 xres[1 - par][:, :, :]).then_inc(out_done[1 - par], 16)
                if is_group(r + 1):
                    wait(sp, out_done[1 - par], 16 * (half + par))
                    sp.dma_start(xres[1 - par][:, :, :], x2_t[bass.ds(GT * (r + 1), GT), :].rearrange("(u p) d -> p u d", p=P)
                                 ).then_inc(xres_in[1 - par], 16)

            rounds(sp, -2, GROUPS, experts, B_FROM, B_TO)
            for par in range(2):
                sp.wait_ge(out_done[par], 16 * GROUPS // 2)

        @block.gpsimd
        def _(pool):
            g = nc.gpsimd
            g.memset(ident[:, :], 0.0).then_inc(const_step, 1)
            g.memset(band[:, :], 0.0).then_inc(const_step, 1)
            g.memset(valid[:, :], 1.0).then_inc(const_step, 1)
            g.iota(iota8[:, :], [[1, K]], base=0, channel_multiplier=0,
                   allow_small_or_imprecise_dtypes=True).then_inc(const_step, 1)
            g.iota(iota_rows[:, :], [[1, P]], base=0, channel_multiplier=0,
                   allow_small_or_imprecise_dtypes=True).then_inc(const_step, 1)
            g.iota(iota_cols[0:P // 2, :, :], [[1, 2 * HK]], base=0, channel_multiplier=0,
                   allow_small_or_imprecise_dtypes=True).then_inc(const_step, 1)
            pool.wait_ge(const_step, 6)
            g.iota(iota_cols[P // 2:P, :, :], [[1, 2 * HK]], base=-HK, channel_multiplier=0,
                   allow_small_or_imprecise_dtypes=True).then_inc(const_step, 1)
            pool.wait_ge(const_step, 7)
            g.affine_select(out=ident[:, :], in_=ident[:, :], compare_op=ALU.not_equal, fill=1.0,
                            base=0, pattern=[[-1, P]], channel_multiplier=1).then_inc(const_step, 1)
            g.affine_select(out=band[:, :], in_=band[:, :], compare_op=ALU.is_ge, fill=FAR,
                            base=W, pattern=[[-1, P]], channel_multiplier=1).then_inc(const_step, 1)
            g.affine_select(out=valid[:, 0:3:2], in_=valid[:, 0:3:2], compare_op=ALU.is_ge, fill=0.0,
                            base=P - W - 1, pattern=[[0, 2]], channel_multiplier=-1).then_inc(const_step, 1)
            pool.wait_ge(const_step, 10)
            g.affine_select(out=band[:, :], in_=band[:, :], compare_op=ALU.is_ge, fill=FAR,
                            base=W, pattern=[[1, P]], channel_multiplier=-1).then_inc(const_step, 1)
            g.affine_select(out=valid[:, 1:3], in_=valid[:, 1:3], compare_op=ALU.is_ge, fill=0.0,
                            base=-W, pattern=[[0, 2]], channel_multiplier=1).then_inc(const_step, 1)
            pool.wait_ge(const_step, 12)
            g.memset(ones[:, :], 1.0).then_inc(const_ready, 1)
            pool.wait_ge(weights_in, 16 * 8)

            def attention(half, par):
                i = 2 * half + par
                if is_step(i - 1):
                    xb = xr[1 - par]
                    wait(pool, xr_in[1 - par], 16 * (half + par))
                    g.tensor_tensor(xb, xb, bv_sb[:, :].unsqueeze(1).broadcast_to([P, NB, H]),
                                    ALU.add).then_inc(xb_ready, 1)
                n = i - 3
                if not is_step(n) or (known(n) and n >= STEPS - 2):
                    return
                l2 = ln2[1 - par].rearrange("p b d -> p (b d)")
                sq_f = sq.rearrange("p b d -> p (b d)")
                wait(pool, ln2_ready, n + 1)
                if known(n) and n == 0:
                    g.tensor_tensor(acc_edge[:, 0, 0, :], l2[:, 0:H], l2[:, H:2 * H], ALU.add).then_inc(stats_added, 1)
                    g.tensor_tensor(sq_f, l2, l2, ALU.mult).then_inc(sq_ready, 1)
                    wait(pool, sq_ready, 1)
                    g.tensor_tensor(acc_edge[:, 0, 1, :], sq_f[:, 0:H], sq_f[:, H:2 * H], ALU.add).then_inc(stats_added, 1)
                elif known(n) and n == 1:
                    g.tensor_copy(acc_mid[:, 0, :], l2).then_inc(stats_added, 1)
                    g.tensor_tensor(acc_mid[:, 1, :], l2, l2, ALU.mult).then_inc(stats_added, 1)
                else:
                    wait(pool, stats_added, 2 * n)
                    g.tensor_tensor(sq_f, l2, l2, ALU.mult).then_inc(sq_ready, 1)
                    g.tensor_tensor(acc_mid[:, 0, :], acc_mid[:, 0, :], l2, ALU.add).then_inc(stats_added, 1)
                    wait(pool, sq_ready, n)
                    g.tensor_tensor(acc_mid[:, 1, :], acc_mid[:, 1, :], sq_f, ALU.add).then_inc(stats_added, 1)

            rounds(pool, 1, STEPS + 1, attention, 6, A_TO)

            def build(half, par):
                r = 2 * half + par
                if not is_group(r + 1):
                    return
                for s_ in range(ST):
                    q, u, j = ST * (r + 1) + s_, s_ // TS, PS * (s_ % TS)
                    wait(pool, hits_ready, q + 1)
                    wait(pool, gate_done, q - 1)
                    g.tensor_tensor(cols_gate[s_ % 2][:, :, :], cols_hot[s_ % 2][:, :, :],
                                    codesT[u][:, 2, j:j + PS].unsqueeze(2).broadcast_to([P, PS, 2 * HK]),
                                    ALU.mult).then_inc(cols_ready, 1)

            rounds(pool, -1, GROUPS - 2, build, B_FROM, B_TO)

        @block.tensor
        def _(pe):
            mm = nc.tensor.matmul
            pe.wait_ge(const_ready, 1)
            def weight_products():
                pe.wait_ge(weights_in, 16 * 8)
                for f in range(HC):
                    for m in range(HC):
                        last = mm(ps_w[:, f, :], wqT_sb[:, m, f * P:(f + 1) * P], wkT_sb[:, m, :],
                                  start=(m == 0), stop=(m == HC - 1))
                last.then_inc(a_done, 1)
                for ps, w, col in ((ps_c, wkT_sb, bq_sb), (ps_u, wqT_sb, bk_sb)):
                    for f in range(HC):
                        for m in range(HC):
                            last = mm(ps[:, f:f + 1], w[:, m, f * P:(f + 1) * P], col[:, m:m + 1],
                                      start=(m == 0), stop=(m == HC - 1))
                pe.wait_ge(bqk_ready, 1)
                for m in range(HC):
                    last = mm(ps_bqk, ones[:, :], bqk[:, m:m + 1], start=(m == 0), stop=(m == HC - 1))
                last.then_inc(weights_done, 1)

            def fold_keys(n):
                c, u0 = n // 2, NH * (n % 2)
                if n == 0:
                    pe.wait_ge(fold_in, 32)
                if n == 1:
                    pe.wait_ge(fold_copied, 1)
                for u in range(u0, u0 + NH):
                    last = mm(ps_fold[n][:, (u - u0) * NK:(u - u0 + 1) * NK], wquery_sb[:, u, c * P:(c + 1) * P],
                              keys_sb[:, u, :], start=True, stop=True)
                last.then_inc(fold_done, 1)

            def transposes(n):
                wait(pe, ln_ready, n + 1)
                for c in range(HC):
                    for b in range(NB):
                        last = nc.tensor.transpose(ps_t[:, c, b, :], ln[:, b, c * P:(c + 1) * P], ident[:, :])
                last.then_inc(t_done, 1)

            def attention(half, par):
                i = 2 * half + par
                if is_step(i):
                    wait(pe, lnT_ready, i + 1)
                    wait(pe, g_ready, i)
                    if known(i) and i == 0:
                        pe.wait_ge(a_ready, 1)
                    for m in range(HC):
                        for c in range(HC):
                            last = mm(ps_g[:, m, :], a_sb[:, c, m * P:(m + 1) * P],
                                      lnT[:, c, :, :].rearrange("p b t -> p (b t)"),
                                      start=(c == 0), stop=(c == HC - 1))
                    last.then_inc(g_done, 1)
                    wait(pe, v_ready, i)
                    if known(i) and i == 0:
                        pe.wait_ge(band_ready, 1)
                    for b in range(NB):
                        for c in range(HC):
                            last = mm(ps_v[b], lnT[:, c, b, :], wvu_sb[:, c, :], start=(c == 0), stop=(c == HC - 1))
                    last.then_inc(v_done, 1)
                if is_step(i - 1):
                    wait(pe, prT_ready, i - 1)
                    wait(pe, p_ready, i)
                    for b in range(NB):
                        last = nc.tensor.transpose(ps_pt[:, b, :], pr[:, b, :], ident[:, :])
                    last.then_inc(pt_done, 1)
                if known(i) and i in (0, 1):
                    fold_keys(i)
                if is_step(i):
                    wait(pe, g_ready, i + 1)
                    for b in range(NB):
                        for c in range(HC):
                            last = mm(ps_s[:, b, :], gT[:, c, b * P:(b + 1) * P], lnT[:, c, b, :],
                                      start=(c == 0), stop=(c == HC - 1))
                    last.then_inc(s_done, 1)
                if is_step(i + 1):
                    transposes(i + 1)
                if is_step(i - 1):
                    if known(i) and i == STEPS:
                        fold_keys(2)
                    wait(pe, prT_ready, i)
                    wait(pe, v_ready, i)
                    wait(pe, x2_ready, i - 1)
                    for b in range(NB):
                        last = mm(ps_o[:, b, :], prT[:, b, :], vu[1 - par][:, b, 0:H], start=True, stop=True)
                    last.then_inc(o_done, 1)

            attention(-1, 1)
            weight_products()
            rounds(pe, 0, STEPS, attention, A_FROM, A_TO)

            def column_sums(cols, kind, at, start, stop):
                for s in range(2):
                    for c in range(HC):
                        last = mm(ps_stat[s][c][:, 0:1], cols(s)[:, at + c * P:at + (c + 1) * P],
                                  valid[:, kind:kind + 1], start=start, stop=stop)
                return last

            pe.wait_ge(stats_added, 2)
            pe.wait_ge(fold_copied, 2)
            column_sums(lambda s: acc_edge[:, 0, s, :], 0, 0, True, False)
            pe.wait_ge(stats_added, 2 * (STEPS - 2))
            for b in range(NB):
                column_sums(lambda s: acc_mid[:, s, :], 2, b * H, False, False)
            pe.wait_ge(last_added, 1)
            column_sums(lambda s: acc_edge[:, 1, s, :], 2, 0, False, False)
            pe.wait_ge(last_added, 2)
            column_sums(lambda s: acc_edge[:, 2, s, :], 1, 0, False, True).then_inc(stat_done, 1)
            fold_keys(3)

            def choice_input(half, par, u):
                r = 2 * half + par
                n = 2 * (r + 2) + u
                if u == 0:
                    wait(pe, rt_read, 2 * (r + 1))
                    if known(r) and r == -1:
                        pe.wait_ge(ct_read, 1)
                    wait(pe, lnb_in[par], 16 * (half + 2))
                else:
                    wait(pe, ct_read, n - 1)
                for c in range(HC):
                    last = nc.tensor.transpose(ps_bt[:, c, :], lnb[par][:, u, c * P:(c + 1) * P], ident[:, :])
                last.then_inc(bt_done, 1)

            def choice_scores(n):
                wait(pe, bt_read, n + 1)
                wait(pe, topi_ready, UNITS * n)
                if known(n) and n == 0:
                    pe.wait_ge(fold_copied, 4)
                for m in range(2):
                    for c in range(HC):
                        last = mm(ps_sim[m][:, :], lnbT[:, c, :], fold[:, c, m * 512:(m + 1) * 512],
                                  start=(c == 0), stop=(c == HC - 1))
                    last.then_inc(sim_done, 1)

            def turn_codes(n):
                wait(pe, codes_ready, n + 1)
                wait(pe, tanh_ready, n + 1)
                wait(pe, bt_read, n + 2 if not known(n) else min(n + 2, TILES))
                if known(n) and n == TILES - 1:
                    pe.wait_ge(rt_read, TILES - 2)
                for a_ in range(3):
                    last = nc.tensor.transpose(ps_ct[:, a_, :], codes[:, a_, :, :].rearrange("p d s -> p (d s)"), ident[:, :])
                last.then_inc(ct_done, 1)

            def product_input(half, par, u):
                r = 2 * half + par
                n = 2 * (r + 1) + u
                if u == 0:
                    wait(pe, ct_read, n + 3 if not known(n) else min(n + 3, TILES))
                    wait(pe, lnr_in, 16 * (r + 2))
                else:
                    wait(pe, rt_read, n)
                for c in range(HC):
                    last = nc.tensor.transpose(ps_bt[:, c, :], lnr[:, u, c * P:(c + 1) * P], ident[:, :])
                last.then_inc(rt_done, 1)

            def add_up(r, s_):
                wait(pe, wgt_ready, ST * r + s_ + 1)
                if s_ == 0:
                    wait(pe, y_added, r)
                    if known(r) and r == 0:
                        pe.wait_ge(up_in, 16)
                for c in range(CS):
                    for u in range(2):
                        last = mm(ps_y[:, u, :], wgt[s_ % 2][:, c, u * P:(u + 1) * P], up[:, CS * s_ + c, :],
                                  start=(s_ == 0 and c == 0 and u == 0),
                                  stop=(s_ == ST - 1 and c == CS - 1 and u == 1))
                last.then_inc(y_done, 1)

            def experts(half, par):
                r = 2 * half + par
                for s_ in range(ST):
                    u = s_ // TS
                    if is_group(r + 2) and s_ % TS == 0:
                        choice_input(half, par, u)
                    if is_group(r + 2) and s_ % TS == 1:
                        choice_scores(2 * (r + 2) + u)
                    if is_group(r + 1) and s_ == CODES_AT[1]:
                        turn_codes(2 * (r + 1) + 1)
                    if is_group(r + 2) and s_ == CODES_AT[0]:
                        turn_codes(2 * (r + 2))
                    if is_group(r + 1) and s_ in INPUT_AT:
                        product_input(half, par, INPUT_AT.index(s_))
                    if is_group(r):
                        d = ST * r + s_
                        if s_ == 0:
                            wait(pe, rt_read, 2 * (r + 1))
                            if known(r) and r == 0:
                                pe.wait_ge(down_in, 16)
                        wait(pe, gel_ready, d - 1)
                        for c in range(CS):
                            for k in range(HC):
                                last = mm(ps_hid[s_ % 2][:, c * GT:(c + 1) * GT], down[:, k, CS * s_ + c, :],
                                          lnT2[par][:, k, :], start=(k == 0), stop=(k == HC - 1))
                        last.then_inc(hid_done, 1)
                    if is_group(r + 1):
                        q = ST * (r + 1) + s_
                        wait(pe, hits_ready, q + 1)
                        wait(pe, cols_ready, q + 1)
                        wait(pe, gate_read, q - 1)
                        for j in range(PS):
                            last = mm(ps_gate[s_ % 2][:, j * 2 * HK:(j + 1) * 2 * HK], rows_hot[s_ % 2][:, j, :],
                                      cols_gate[s_ % 2][:, j, :], start=True, stop=True)
                        last.then_inc(gate_done, 1)
                    if s_ > 0 and is_group(r):
                        add_up(r, s_ - 1)
                    if s_ == 0 and is_group(r - 1):
                        add_up(r - 1, ST - 1)
                    if known(r) and r == GROUPS:
                        break

            rounds(pe, -2, GROUPS, experts, B_FROM, B_TO)

        @block.scalar
        def _(act):
            a = nc.scalar.activation
            def copy_products():
                act.wait_ge(a_done, 1)
                a(a_sb[:, :, :], ps_w, ACT.Copy, scale=SCALE)
                act.wait_ge(weights_done, 1)
                a(c_sb[:, :], ps_c, ACT.Copy, scale=SCALE)
                a(wvu_sb[:, :, H], ps_u, ACT.Copy, scale=SCALE).then_inc(a_ready, 1)

            def copy_fold(n):
                c, u0 = n // 2, NH * (n % 2)
                act.wait_ge(fold_done, n + 1)
                a(fold[:, c, u0 * NK:(u0 + NH) * NK], ps_fold[n][:, :], ACT.Copy).then_inc(fold_copied, 1)

            def attention(half, par):
                i = 2 * half + par
                if is_step(i):
                    wait(act, g_done, i + 1)
                    if known(i) and i == 0:
                        act.wait_ge(a_ready, 1)
                    for m in range(HC):
                        last = a(gT[:, m, :], ps_g[:, m, :], ACT.Identity, bias=c_sb[:, m:m + 1])
                    last.then_inc(g_ready, 1)
                    wait(act, v_done, i + 1)
                    wait(act, o_done, i - 1)
                    for b in range(NB):
                        last = a(vu[par][:, b, :], ps_v[b], ACT.Copy)
                    last.then_inc(v_ready, 1)
                if is_step(i - 1):
                    wait(act, pt_done, i)
                    a(prT, ps_pt, ACT.Copy).then_inc(prT_ready, 1)
                if known(i) and i in (0, 1):
                    copy_fold(i)
                if is_step(i + 1):
                    wait(act, s_done, i + 1)
                    wait(act, t_done, i + 2)
                    a(lnT, ps_t, ACT.Copy).then_inc(lnT_ready, 1)
                if is_step(i):
                    wait(act, nmax_ready, i + 1)
                    for b in range(NB):
                        last = a(pr[:, b, :], sm[:, b, :], ACT.Exp, bias=nmax[:, b:b + 1],
                                 accum_out=rsum[par][:, b:b + 1])
                    last.then_inc(p_ready, 1)

            attention(-1, 1)
            copy_products()
            rounds(act, 0, STEPS, attention, A_FROM, A_TO)
            copy_fold(2)
            copy_fold(3)

            def experts(half, par):
                r = 2 * half + par
                for s_ in range(ST):
                    u = s_ // TS
                    if is_group(r + 2) and s_ % TS == 0:
                        n = 2 * (r + 2) + u
                        wait(act, bt_done, n + 1)
                        if known(n) and n == 0:
                            act.wait_ge(norm_ready, 1)
                        wait(act, sim_done, 2 * n)
                        for c in range(HC):
                            last = a(lnbT[:, c, :], ps_bt[:, c, :], ACT.Identity,
                                     bias=shift[:, c:c + 1], scale=factor[:, c:c + 1])
                        last.then_inc(bt_read, 1)
                    if is_group(r + 1) and s_ == CODES_AT[1]:
                        copy_codes(2 * (r + 1) + 1, 1)
                    if is_group(r + 2) and s_ == CODES_AT[0]:
                        copy_codes(2 * (r + 2), 0)
                    if is_group(r + 1) and s_ in INPUT_AT:
                        v_ = INPUT_AT.index(s_)
                        wait(act, rt_done, 2 * (r + 1) + v_ + 1)
                        wait(act, hid_done, ST * r)
                        a(lnT2[1 - par][:, :, v_ * P:(v_ + 1) * P], ps_bt, ACT.Copy).then_inc(rt_read, 1)
                    if is_group(r):
                        d = ST * r + s_
                        wait(act, hid_done, d + 1)
                        wait(act, wgt_ready, d - 1)
                        a(gel[s_ % 2][:, :, :].rearrange("p c t -> p (c t)"), ps_hid[s_ % 2][:, :],
                          ACT.Gelu).then_inc(gel_ready, 1)
                    if is_group(r + 1):
                        q, j = ST * (r + 1) + s_, PS * (s_ % TS)
                        wait(act, gate_done, q + 1)
                        if s_ == 0:
                            wait(act, wgt_ready, ST * r)
                            if known(r) and r == -1:
                                act.wait_ge(lnr_in, 16)
                        grid = gates[1 - par].rearrange("p c (u h j) -> p u j h c", u=2, h=2)
                        a(grid[:, u, j:j + PS, :, :],
                          ps_gate[s_ % 2][:, :].rearrange("p (j h c) -> p j h c", j=PS, h=2), ACT.Copy).then_inc(gate_read, 1)
                    if is_group(r + 2) and s_ % TS == TANH_AT:
                        n = 2 * (r + 2) + u
                        wait(act, best_ready, NH * (n + 1))
                        wait(act, ct_done, n)
                        a(codes[:, 2, :, :], best[:, :, :].rearrange("p h k -> p (h k)").unsqueeze(1).broadcast_to([P, 2, SEL]),
                          ACT.Tanh, scale=0.5).then_inc(tanh_ready, 1)

            def copy_codes(n, u):
                wait(act, ct_done, n + 1)
                wait(act, hits_ready, TS * (n - 1))
                wait(act, cols_ready, TS * (n - 1))
                hp = P // 2
                for h in range(2):
                    side = slice(h * hp, (h + 1) * hp)
                    a(codesT[u][side, 0:2, :], ps_ct[side, 0:2, side], ACT.Copy)
                    last = a(codesT[u][side, 2, :], ps_ct[side, 2, side], ACT.Identity, bias=1.0)
                last.then_inc(ct_read, 1)

            rounds(act, -2, GROUPS - 1, experts, B_FROM, B_TO)

        @block.vector
        def _(dve):
            v = nc.vector
            v.memset(mv[:, :, :], 1.0).then_inc(mv_set, 1)
            dve.wait_ge(mv_set, 1)

            def root(var, y, sa, sb_, count, base, steps, between=()):
                fill = list(between)
                done = [0]

                def then(ins):
                    ins.then_inc(count, 1)
                    done[0] += 1
                    if fill:
                        fill.pop(0)()
                    wait(dve, count, base + done[0])

                then(v.tensor_scalar(y.bitcast(u32), var.bitcast(u32), -0.5, float(0x5F1FFFF9), ALU.mult, ALU.add))
                for n in range(steps):
                    ka, kb = (-0.703952253, 0.703952253 * 2.38924456) if n == 0 else (-0.5, 1.5)
                    then(v.tensor_tensor(sa, y, y, ALU.mult))
                    then(v.scalar_tensor_tensor(sb_, sa, ka, var, ALU.mult, ALU.mult))
                    then(v.scalar_tensor_tensor(y, sb_, kb, y, ALU.add, ALU.mult))
                for f in fill:
                    f()

            def last_sums(n, e):
                l2 = ln2[n % 2].rearrange("p b d -> p (b d)")
                sq_f = sq.rearrange("p b d -> p (b d)")

                def squares():
                    dve.wait_ge(stats_added, 2 * (STEPS - 2))
                    dve.wait_ge(ln2_ready, n + 1)
                    dve.wait_ge(last_added, e - 1) if e > 1 else None
                    v.tensor_tensor(sq_f, l2, l2, ALU.mult).then_inc(last_step, 1)

                def sums():
                    v.tensor_tensor(acc_edge[:, e, 0, :], l2[:, 0:H], l2[:, H:2 * H], ALU.add)

                def sums_of_squares():
                    dve.wait_ge(last_step, e)
                    v.tensor_tensor(acc_edge[:, e, 1, :], sq_f[:, 0:H], sq_f[:, H:2 * H], ALU.add).then_inc(last_added, 1)

                return [squares, sums, sums_of_squares]

            def attention(half, par):
                i = 2 * half + par
                fill = []

                def reciprocal():
                    wait(dve, p_ready, i - 1)
                    v.reciprocal(rcp[:, :], rsum[par][:, :]).then_inc(rcp_ready, 1)

                def output(b):
                    if b == 0:
                        wait(dve, rcp_ready, i - 1)
                        wait(dve, o_done, i - 1)
                        wait(dve, xb_ready, i - 1)
                        wait(dve, x2_out[par], 16 * (half - 1))
                    ins = v.scalar_tensor_tensor(x2[par][:, b, :], ps_o[:, b, :], rcp[:, b:b + 1],
                                                 xr[par][:, b, :], ALU.mult, ALU.add)
                    if b == NB - 1:
                        ins.then_inc(x2_ready, 1)

                def x2_stats(b):
                    if b == 0:
                        wait(dve, x2_ready, i - 1)
                    ins = v.bn_stats(bst[:, NB + b, :], x2[par][:, b, :])
                    if b == NB - 1:
                        ins.then_inc(x2_seen, 1)

                def xa_stats(b):
                    if b == 0:
                        wait(dve, xa_in[par], 16 * (half + 2))
                    ins = v.bn_stats(bst[:, b, :], xa[par][:, b, :])
                    if b == NB - 1:
                        ins.then_inc(xa_seen, 1)

                if is_step(i - 2):
                    fill += [reciprocal, lambda: output(0), lambda: output(1)]
                if is_step(i + 2):
                    fill += [lambda: xa_stats(0), lambda: xa_stats(1)]
                if is_step(i - 2):
                    fill += [lambda: x2_stats(0), lambda: x2_stats(1)]
                if known(i) and i == STEPS + 2:
                    fill += last_sums(STEPS - 2, 1)
                if is_step(i + 1) or is_step(i - 3):
                    wait(dve, veps_ready, i + 2)
                    root(veps[:, :], rstd[:, :], root_a[:, :], root_b[:, :], root_step, ROOT * (i + 1), 2, fill)
                else:
                    for f in fill:
                        f()
                if is_step(i + 1):
                    wait(dve, t_done, i + 1)
                    for b in range(NB):
                        last = v.tensor_scalar(ln[:, b, :], xa[1 - par][:, b, :], mv[:, b, 0:1], rstd[:, b:b + 1],
                                               ALU.subtract, ALU.mult)
                    last.then_inc(ln_ready, 1)
                if is_step(i - 3):
                    wait(dve, ln2_out[1 - par], 16 * (half - 2 + par))
                    wait(dve, stats_added, 2 * (i - 4) if not known(i) else 2 * min(i - 4, STEPS - 2))
                    for b in range(NB):
                        last = v.tensor_scalar(ln2[1 - par][:, b, :], x2[1 - par][:, b, :], mv[:, NB + b, 0:1],
                                               rstd[:, NB + b:NB + b + 1], ALU.subtract, ALU.mult)
                    last.then_inc(ln2_ready, 1)
                if is_step(i):
                    if known(i) and i == 0:
                        mask_constant()
                    wait(dve, s_done, i + 1)
                    wait(dve, v_ready, i + 1)
                    for b in range(NB):
                        last = v.scalar_tensor_tensor(sm[:, b, :], ps_s[:, b, :], vu[par][:, b, H:H + 1],
                                                      band[:, :], ALU.add, ALU.add)
                    last.then_inc(masked, 1)
                ahead, behind = is_step(i + 2), is_step(i - 2)
                if ahead or behind:
                    if is_step(i + 1):
                        wait(dve, ln_ready, i + 2)
                    if is_step(i - 3):
                        wait(dve, ln2_ready, i - 2)
                    if ahead:
                        wait(dve, xa_seen, i + 3)
                    if behind:
                        wait(dve, x2_seen, i - 1)
                    dve.nop(nofuse=True)
                    for b in range(0 if ahead else NB, 2 * NB if behind else NB):
                        last = v.bn_aggr(mv[:, b, :], bst[:, b, :])
                    last.then_inc(mv_ready, 1)
                if is_step(i):
                    wait(dve, masked, i + 1)
                    v.tensor_reduce(nmax[:, :], sm, AX.X, ALU.max, negate=True).then_inc(nmax_ready, 1)
                if ahead or behind:
                    wait(dve, mv_ready, i + 3)
                    v.tensor_scalar(veps[:, :], mv[:, :, 1], EPS, None, ALU.add).then_inc(veps_ready, 1)

            def mask_constant():
                dve.wait_ge(weights_done, 1)
                v.tensor_scalar(bqk_sb[:, :], ps_bqk, SCALE, None, ALU.mult).then_inc(bqk_scaled, 1)
                dve.wait_ge(bqk_scaled, 1)
                v.tensor_scalar(band[:, :], band[:, :], bqk_sb[:, :], None, ALU.add).then_inc(band_ready, 1)
                dve.wait_ge(band_ready, 1)

            ROOT = 7
            attention(-1, 0)
            attention(-1, 1)
            dve.wait_ge(const_ready, 1)
            dve.wait_ge(weights_in, 16 * 8)
            v.tensor_tensor(bqk[:, :], bq_sb[:, :], bk_sb[:, :], ALU.mult).then_inc(bqk_ready, 1)
            rounds(dve, 0, STEPS + 2, attention, 6, A_TO)

            for f in last_sums(STEPS - 1, 2):
                f()

            count = [0]

            def then(*group):
                count[0] += 1
                group[-1].then_inc(bs_step, 1)
                dve.wait_ge(bs_step, count[0])

            dve.wait_ge(stat_done, 1)
            then(*[v.tensor_scalar(mean[:, c:c + 1], ps_stat[0][c][:, 0:1], 1.0 / TOKENS, None, ALU.mult) for c in range(HC)],
                 *[v.tensor_scalar(ex2[:, c:c + 1], ps_stat[1][c][:, 0:1], 1.0 / TOKENS, EPS, ALU.mult, ALU.add) for c in range(HC)])
            then(v.tensor_tensor(msq, mean, mean, ALU.mult))
            then(v.tensor_tensor(bvar, ex2, msq, ALU.subtract))
            root(bvar, inv, bs_a, bs_b, bs_step, count[0], 3)
            count[0] += 10
            then(v.tensor_tensor(factor, inv, gamma_sb[:, :], ALU.mult))
            then(v.tensor_tensor(msq, mean, factor, ALU.mult))
            v.tensor_tensor(shift, beta_sb[:, :], msq, ALU.subtract).then_inc(norm_ready, 1)

            def best_keys(n, p):
                wait_apart(dve, sim_done, 2 * n + p + 1)
                for h in range(NH):
                    v.max(top[:, p * NH + h, :], ps_sim[p][:, h * NK:(h + 1) * NK]).then_inc(top_ready, 1)
                wait_apart(dve, top_ready, UNITS * n + NH * (p + 1))
                for h in range(NH):
                    v.max_index(topi[:, p * NH + h, :], top[:, p * NH + h, :],
                                ps_sim[p][:, h * NK:(h + 1) * NK]).then_inc(topi_ready, 1)

            def own(sem_, value):
                def then(*group):
                    group[-1].then_inc(sem_, 1)
                    wait_apart(dve, sem_, value)
                return then

            def best_pairs(n):
                first = top[:, 0:NH, :].unsqueeze(3).broadcast_to([P, NH, K, K])
                second = top[:, NH:UNITS, :].unsqueeze(2).broadcast_to([P, NH, K, K])
                wait(dve, tanh_ready, n)
                own(pair_ready, n + 1)(v.tensor_tensor(pair[:, :, :].rearrange("p h (i j) -> p h i j", i=K), first, second, ALU.add))
                for h in range(NH):
                    v.max(best[:, h, :], pair[:, h, :]).then_inc(best_ready, 1)
                wait_apart(dve, best_ready, NH * (n + 1))
                own(besti_ready, n + 1)(*[v.max_index(besti[:, K * h:K * (h + 1)], best[:, h, :], pair[:, h, :]) for h in range(NH)])

            def name_experts(n):
                own(pos_ready, n + 1)(
                    v.tensor_scalar(pos[:, 0, :], besti[:, :], 3, None, ALU.logical_shift_right),
                    v.tensor_scalar(pos[:, 1, :], besti[:, :], K - 1, None, ALU.bitwise_and))
                own(hot_ready, n + 1)(
                    v.tensor_tensor(hot[:, :, :, :], pos[:, :, :].unsqueeze(3).broadcast_to([P, 2, SEL, K]),
                                    iota8[:, :].unsqueeze(1).unsqueeze(1).broadcast_to([P, 2, SEL, K]), ALU.is_equal))
                wait(dve, topi_ready, UNITS * (n + 1))
                own(hotv_ready, n + 1)(
                    *[v.tensor_tensor(hot[:, p, :, :].rearrange("p (h k) m -> p h k m", h=NH),
                                      hot[:, p, :, :].rearrange("p (h k) m -> p h k m", h=NH),
                                      topi[:, p * NH:(p + 1) * NH, :].unsqueeze(2).broadcast_to([P, NH, K, K]),
                                      ALU.mult) for p in range(2)])
                own(part_ready, n + 1)(v.tensor_reduce(part[:, :, :], hot[:, :, :, :], AX.X, ALU.add))
                own(upper_ready, n + 1)(v.tensor_scalar(upper[:, :], part[:, 1, :], float(HK), None, ALU.is_ge))
                wait(dve, ct_done, n)
                twice = [x_.unsqueeze(1).broadcast_to([P, 2, SEL]) for x_ in (upper[:, :], part[:, 0, :], part[:, 1, :])]
                v.scalar_tensor_tensor(codes[:, 0, :, :], twice[0], float(NK), twice[1], ALU.mult, ALU.add)
                v.scalar_tensor_tensor(codes[:, 1, :, :], twice[0], -float(HK), twice[2], ALU.mult, ALU.add).then_inc(codes_ready, 1)

            def finish(r, half, par):
                wait(dve, y_done, ST * (r + 1))
                wait(dve, xres_in[par], 16 * (half + 1))
                v.tensor_tensor(xres[par][:, :, :], ps_y, xres[par][:, :, :], ALU.add).then_inc(y_added, 1)

            def one_hots(q, n, s_):
                u, j = s_ // TS, PS * (s_ % TS)
                if s_ % TS == 0:
                    wait(dve, ct_read, n + 1)
                wait(dve, gate_done, q - 1)
                wait(dve, cols_ready, q - 1)
                for hits, iota, a_ in ((rows_hot, iota_rows[:, :], 0), (cols_hot, iota_cols[:, :, :].rearrange("p h c -> p (h c)"), 1)):
                    shape = hits[s_ % 2].shape
                    last = v.tensor_tensor(hits[s_ % 2][:, :, :], iota.unsqueeze(1).broadcast_to(shape),
                                           codesT[u][:, a_, j:j + PS].unsqueeze(2).broadcast_to(shape), ALU.is_equal)
                last.then_inc(hits_ready, 1)

            def experts(half, par):
                r = 2 * half + par
                for s_ in range(ST):
                    u = s_ // TS
                    if s_ == 1 and is_group(r - 1):
                        finish(r - 1, half if par else half - 1, 1 - par)
                    if is_group(r):
                        d = ST * r + s_
                        wait(dve, gel_ready, d + 1)
                        if s_ == 0:
                            wait(dve, gate_read, ST * (r + 1))
                        wait(dve, y_done, d - 1)
                        v.scalar_tensor_tensor(wgt[s_ % 2][:, :, :], gel[s_ % 2][:, :, :], 0.5,
                                               gates[par][:, CS * s_:CS * (s_ + 1), :], ALU.mult, ALU.mult).then_inc(wgt_ready, 1)
                    g, b = (r + 1, s_ + 1) if s_ < ST - 1 else (r + 2, 0)
                    if is_group(g):
                        one_hots(ST * g + b, 2 * g + b // TS, b)
                    if is_group(r + 2):
                        n = 2 * (r + 2) + u
                        if s_ % TS in KEYS_AT:
                            best_keys(n, KEYS_AT.index(s_ % TS))
                        if s_ % TS == PAIRS_AT:
                            best_pairs(n)
                        if s_ % TS == NAMES_AT:
                            name_experts(n)

            rounds(dve, -2, GROUPS - 1, experts, B_FROM, B_TO)
            finish(GROUPS - 1, (GROUPS - 1) // 2, 1)


def kernel(L0_attn_sequence_output, L0_attn_Wq, L0_attn_bq, L0_attn_Wk, L0_attn_bk, L0_attn_Wv, L0_attn_bv,
           L0_ffn_bn_gamma, L0_ffn_bn_beta, L0_ffn_w_q, L0_ffn_keys_p, L0_ffn_down, L0_ffn_up):
    import numpy as np
    import concourse.bacc as bacc
    from concourse.bass_utils import run_bass_kernel_spmd

    keys = np.asarray(L0_ffn_keys_p)
    nh, nk, halves, kd = keys.shape

    def by_chunk(table):
        t = np.asarray(table)[:nk * nk].reshape(nk, 2, nk // 2, -1)
        return t.transpose(2, 1, 0, 3).reshape(nk * nk, -1)

    arrays = {
        "x": L0_attn_sequence_output, "wq_t": np.asarray(L0_attn_Wq).T, "bq": L0_attn_bq, "wk_t": np.asarray(L0_attn_Wk).T, "bk": L0_attn_bk,
        "wv": L0_attn_Wv, "bv": L0_attn_bv, "gamma": L0_ffn_bn_gamma, "beta": L0_ffn_bn_beta,
        "w_query": L0_ffn_w_q,
        "keys_t": keys.transpose(3, 2, 0, 1).reshape(kd, halves * nh, nk),
        "down_t": by_chunk(L0_ffn_down).T,
        "up_c": by_chunk(L0_ffn_up),
    }
    arrays = {n: np.ascontiguousarray(a) for n, a in arrays.items()}
    nc = bacc.Bacc("TRN2", target_bir_lowering=False, num_devices=1)
    args = [nc.dram_tensor(n, a.shape, mybir.dt.from_np(a.dtype), kind="ExternalInput").ap()
            for n, a in arrays.items()]
    shape = arrays["x"].shape
    out = nc.dram_tensor("out", shape, mybir.dt.float32, kind="ExternalOutput").ap()
    window_attention_peer_kernel(nc, *args, out)
    r = run_bass_kernel_spmd(nc, [arrays], core_ids=[0])
    return r.results[0]["out"]
```

```python
import concourse.bass as bass
from concourse import mybir
from contextlib import ExitStack



def window_attention_peer_kernel(
    nc: bass.Bass,
    x: bass.AP,
    wq_t: bass.AP,
    bq: bass.AP,
    wk_t: bass.AP,
    bk: bass.AP,
    wv: bass.AP,
    bv: bass.AP,
    gamma: bass.AP,
    beta: bass.AP,
    w_query: bass.AP,
    keys_t: bass.AP,
    down_t: bass.AP,
    up_c: bass.AP,
    out: bass.AP,
):
    f32 = mybir.dt.float32
    u32 = mybir.dt.uint32
    bf16 = mybir.dt.bfloat16
    f32r = mybir.dt.float32r
    ALU = mybir.AluOpType
    ACT = mybir.ActivationFunctionType
    AX = mybir.AxisListType

    P = 128
    NB, S, H = x.shape
    HC = H // P
    W = 2
    QS = P - 2 * W
    STEPS = (S - P) // QS + 1
    assert (STEPS - 1) * QS + P == S
    SCALE = float(H) ** -0.5
    EPS = 1e-5
    FAR = -1.0e30
    NH = 8
    K = 8
    NK = keys_t.shape[2]
    UNITS = 2 * NH
    TOKENS = NB * S
    TILES = TOKENS // P
    GT = 2 * P
    GROUPS = TOKENS // GT
    SEL = NH * K
    CH = NK * NK // P
    HK = NK // 2
    ST = 16
    CS, PS = CH // ST, P // ST
    TS = ST // 2

    ctx = ExitStack()
    with ctx:
        def sb(name, shape, dt=f32):
            return ctx.enter_context(nc.sbuf_tensor(name, shape, dt))

        def sem(name):
            return ctx.enter_context(nc.semaphore(name))

        x_s = x.rearrange("b s d -> s b d")
        x2_d = nc.dram_tensor("x2_scratch", (NB, S, H), f32, kind="Internal").ap()
        ln2_d = nc.dram_tensor("ln2_scratch", (NB, S, H), f32, kind="Internal").ap()
        x2_s = x2_d.rearrange("b s d -> s b d")
        ln2_s = ln2_d.rearrange("b s d -> s b d")
        x2_t = x2_d.rearrange("b s d -> (b s) d")
        ln2_t = ln2_d.rearrange("b s d -> (b s) d")
        out_t = out.rearrange("b s d -> (b s) d")
        up_lo_d = nc.dram_tensor("up_lo_scratch", (ST, P, CS * H), f32, kind="Internal").ap()

        ident = sb("ident", [P, P])
        valid = sb("valid", [P, 3])
        iota8 = sb("iota8", [P, K])
        iota_rows = sb("iota_rows", [P, P, PS], bf16)
        iota_cols = sb("iota_cols", [P, 2 * HK, PS], bf16)
        c_sb = sb("c_sb", [P, HC])
        bqk = sb("bqk", [P, HC])
        bqk_sb = sb("bqk_sb", [P, 1])
        bq_sb = sb("bq_sb", [P, HC])
        bk_sb = sb("bk_sb", [P, HC])
        gamma_sb = sb("gamma_sb", [P, HC])
        beta_sb = sb("beta_sb", [P, HC])
        fold = sb("fold", [P, HC, UNITS * NK])

        bst = sb("bst", [P, 4, 6])
        mv = sb("mv", [P, 4, 2])
        veps = sb("veps", [P, 4])
        rstd = sb("rstd", [P, 4])
        root_a = sb("root_a", [P, 4])
        root_b = sb("root_b", [P, 4])
        nmax = sb("nmax", [P, NB])
        rsum = [sb(f"rsum{i}", [P, NB]) for i in range(2)]
        rcp = sb("rcp", [P, NB])
        bs = sb("bs", [P, 9, HC])
        mean, ex2, msq, bvar, inv, bs_a, bs_b, factor, shift = (bs[:, n, :] for n in range(9))

        down_hi = sb("down_hi", [P, HC * CH * P], f32r)
        down_lo = sb("down_lo", [P, HC * CH * P], f32r)
        PIECE = HC * CH * P // ST
        lnb = [sb(f"lnb{i}", [P, 2, H]) for i in range(2)]
        lnr = sb("lnr", [P, 2, H])
        lnbT = sb("lnbT", [P, HC, P])
        ln_hi = [sb(f"ln_hi{i}", [P, HC, GT], f32r) for i in range(2)]
        ln_lo = [sb(f"ln_lo{i}", [P, HC, GT], f32r) for i in range(2)]
        xres = [sb(f"xres{i}", [P, 2, H]) for i in range(2)]
        top = sb("top", [P, UNITS, K])
        topi = sb("topi", [P, UNITS, K], u32)
        best = sb("best", [P, NH, K])
        besti = sb("besti", [P, SEL], u32)
        pos = sb("pos", [P, 2, SEL], u32)
        hot = sb("hot", [P, 2, SEL, K])
        pair = sb("pair", [P, NH, K * K])
        part = sb("part", [P, 2, SEL])
        upper = sb("upper", [P, SEL])
        codes = sb("codes", [P, 3, 2, SEL])
        codesT = [sb(f"codesT{i}", [P, 2, P // 2], bf16) for i in range(2)]
        gateT = [sb(f"gateT{i}", [P, P // 2]) for i in range(2)]
        rest = sb("rest", [P, P // 2])
        gate3 = [sb(f"gate3{i}", [P, 3, P // 2], bf16) for i in range(2)]
        rows_hot = [sb(f"rows_hot{i}", [P, P, PS], bf16) for i in range(2)]
        cols_hot = [sb(f"cols_hot{i}", [P, 2 * HK, PS], bf16) for i in range(2)]
        cols_gate = [sb(f"cols_gate{i}", [P, 3, 2 * HK, PS], bf16) for i in range(2)]
        gel = [sb(f"gel{i}", [P, CS, GT]) for i in range(2)]
        wgt = [sb(f"wgt{i}", [P, CS, GT]) for i in range(2)]


        early = ExitStack()
        flat = early.enter_context(nc.sbuf_tensor("flat", [P, 2 * CH * H + 8 * CS * GT], f32))[:, :]
        spot = [0]

        def shared(*dims):
            n = 1
            for d in dims:
                n *= d
            v = flat[:, spot[0]:spot[0] + n]
            spot[0] += n
            assert spot[0] <= flat.shape[1]
            names = "abcd"[:len(dims)]
            if len(dims) == 1:
                return v
            return v.rearrange(f"p ({' '.join(names)}) -> p {' '.join(names)}",
                               **{c: d for c, d in zip(names, dims)})

        ones = shared(P)
        band = shared(P)
        wquery_sb = shared(UNITS, H)
        keys_sb = shared(UNITS, NK)
        a_sb = shared(HC, H)
        wvu_sb = shared(HC, H + 1)
        bv_sb = shared(H)
        wqT_sb = shared(HC, H)
        wkT_sb = shared(HC, H)
        xa = [shared(NB, H) for _ in range(2)]
        xr = [shared(NB, H) for _ in range(2)]
        ln = shared(NB, H)
        lnT = shared(HC, NB, P)
        gT = shared(HC, NB * P)
        vu = [shared(NB, H + 1) for _ in range(2)]
        sm = shared(NB, P)
        pr = shared(NB, P)
        prT = shared(NB, P)
        x2 = [shared(NB, H) for _ in range(2)]
        ln2 = [shared(NB, H) for _ in range(2)]
        sq = pair[:, :, :].rearrange("p (b h) k -> p b (h k)", b=NB)
        acc_mid = hot[:, :, :, :].rearrange("p a s k -> p a (s k)")
        acc_edge = shared(3, 2, H)
        early.close()

        up_hi = sb("up_hi", [P, CH * H], f32r)
        up_lo = [sb(f"up_lo{i}", [P, CS * H], f32r) for i in range(4)]
        wgt_hi = [sb(f"wgt_hi{i}", [P, CS, GT], f32r) for i in range(2)]
        wgt_lo = [sb(f"wgt_lo{i}", [P, CS, GT], f32r) for i in range(2)]
        grid = sb("grid", [P, CH * GT])[:, :].rearrange("p (a b c t) -> p a b c t", a=ST, b=ST, c=CS)

        bank = [ctx.enter_context(nc.psum_tensor(f"bank{i}", [P, 512], f32)) for i in range(8)]
        ps_t = bank[0][:, :].rearrange("p (c b t) -> p c b t", c=HC, b=NB)
        ps_g = bank[1][:, :].rearrange("p (m t) -> p m t", m=HC)
        ps_v = [bank[3][:, 0:H + 1], bank[2][:, 0:H + 1]]
        ps_s = bank[4][:, 0:NB * P].rearrange("p (b t) -> p b t", b=NB)
        ps_pt = bank[5][:, 0:NB * P].rearrange("p (b t) -> p b t", b=NB)
        ps_o = bank[6][:, :].rearrange("p (b d) -> p b d", b=NB)
        ps_w = bank[7][:, 0:HC * H].rearrange("p (c n) -> p c n", c=HC)
        ps_c = bank[1][:, 0:HC]
        ps_u = bank[3][:, 0:HC]
        ps_bqk = bank[2][:, 0:1]
        ps_fold = [bank[7], bank[7], bank[1], bank[3]]
        ps_stat = [[bank[2], bank[4]], [bank[5], bank[7]]]
        ps_bt = bank[0][:, 0:HC * P].rearrange("p (c t) -> p c t", c=HC)
        ps_ct = bank[0][:, 0:3 * P].rearrange("p (a t) -> p a t", a=3)
        ps_sim = [bank[1], bank[2]]
        ps_hid = [bank[3], bank[4]]
        ps_gate = [bank[5], bank[6]]
        ps_y = bank[7][:, :].rearrange("p (u d) -> p u d", u=2)

        piece = [t[:, :, :].rearrange("p c t -> p (c t)") for t in gel + wgt]
        hi4, lo4 = [t[:, :].rearrange("p (k c e) -> p k c e", k=HC, c=CH) for t in (down_hi, down_lo)]

        weights_in = sem("weights_in")
        fold_in = sem("fold_in")
        xa_in = [sem(f"xa_in{i}") for i in range(2)]
        xr_in = [sem(f"xr_in{i}") for i in range(2)]
        x2_out = [sem(f"x2_out{i}") for i in range(2)]
        ln2_out = [sem(f"ln2_out{i}") for i in range(2)]
        lnb_in = [sem(f"lnb_in{i}") for i in range(2)]
        xres_in = [sem(f"xres_in{i}") for i in range(2)]
        lnr_in = sem("lnr_in")
        table_in = [sem(f"table_in{i}") for i in range(4)]
        lo_out = [sem(f"lo_out{i}") for i in range(4)]
        lo_in = [sem(f"lo_in{i}") for i in range(4)]
        out_done = [sem(f"out_done{i}") for i in range(2)]
        const_step = sem("const_step")
        const_ready = sem("const_ready")
        mv_set = sem("mv_set")
        xa_seen = sem("xa_seen")
        x2_seen = sem("x2_seen")
        mv_ready = sem("mv_ready")
        veps_ready = sem("veps_ready")
        root_step = sem("root_step")
        xb_ready = sem("xb_ready")
        rcp_ready = sem("rcp_ready")
        x2_ready = sem("x2_ready")
        ln_ready = sem("ln_ready")
        ln2_ready = sem("ln2_ready")
        v_ready = sem("v_ready")
        masked = sem("masked")
        nmax_ready = sem("nmax_ready")
        g_ready = sem("g_ready")
        prT_ready = sem("prT_ready")
        lnT_ready = sem("lnT_ready")
        p_ready = sem("p_ready")
        t_done = sem("t_done")
        g_done = sem("g_done")
        v_done = sem("v_done")
        pt_done = sem("pt_done")
        s_done = sem("s_done")
        o_done = sem("o_done")
        sq_ready = sem("sq_ready")
        stats_added = sem("stats_added")
        weights_done = sem("weights_done")
        bqk_ready = sem("bqk_ready")
        bqk_scaled = sem("bqk_scaled")
        a_done = sem("a_done")
        a_ready = sem("a_ready")
        band_ready = sem("band_ready")
        fold_done = sem("fold_done")
        fold_copied = sem("fold_copied")
        last_step = sem("last_step")
        last_added = sem("last_added")
        stat_done = sem("stat_done")
        bs_step = sem("bs_step")
        norm_ready = sem("norm_ready")
        bt_done = sem("bt_done")
        bt_read = sem("bt_read")
        sim_done = sem("sim_done")
        top_ready = sem("top_ready")
        topi_ready = sem("topi_ready")
        pair_ready = sem("pair_ready")
        best_ready = sem("best_ready")
        besti_ready = sem("besti_ready")
        pos_ready = sem("pos_ready")
        hot_ready = sem("hot_ready")
        hotv_ready = sem("hotv_ready")
        part_ready = sem("part_ready")
        upper_ready = sem("upper_ready")
        codes_ready = sem("codes_ready")
        tanh_ready = sem("tanh_ready")
        ct_done = sem("ct_done")
        ct_read = sem("ct_read")
        split_step = sem("split_step")
        rt_done = sem("rt_done")
        rt_read = sem("rt_read")
        rt_split = sem("rt_split")
        table_rounded = sem("table_rounded")
        table_split = sem("table_split")
        hits_ready = sem("hits_ready")
        first_ready = sem("first_ready")
        cols_ready = sem("cols_ready")
        gate_done = sem("gate_done")
        gate_read = sem("gate_read")
        hid_done = sem("hid_done")
        gel_ready = sem("gel_ready")
        wgt_ready = sem("wgt_ready")
        wgt_rounded = sem("wgt_rounded")
        wgt_split = sem("wgt_split")
        y_done = sem("y_done")
        y_added = sem("y_added")

        block = ctx.enter_context(nc.Block())

        def known(i):
            return isinstance(i, int)

        def is_step(i):
            return not known(i) or 0 <= i < STEPS

        def is_group(g):
            return not known(g) or 0 <= g < GROUPS

        def wait(eng, s, value):
            if not known(value) or value > 0:
                eng.wait_ge(s, value)

        def wait_apart(eng, s, value):
            if not known(value) or value > 0:
                eng.wait_ge(s, value)
                eng.nop(nofuse=True)

        def kept_rows(n):
            edge = known(n)
            return (0 if edge and n == 0 else W), (P if edge and n == STEPS - 1 else P - W)

        def rounds(eng, first, last, body, regular_from, regular_to):
            for i in range(first, regular_from):
                body(i // 2, i % 2)
            with eng.Fori(regular_from // 2, (regular_to + 1) // 2) as half:
                body(half, 0)
                body(half, 1)
            for i in range(regular_to + 1, last + 1):
                body(i // 2, i % 2)

        A_FROM, A_TO = 4, 29
        CODES_AT = (TS + 2, 2)
        INPUT_AT = (TS + 4, TS + 6)
        SPLIT_AT = (TS + 5, 5)
        TANH_AT = 7
        DVE_PARTS = 2
        B_FROM, B_TO = 2, 27

        @block.sync
        def _(sp):
            def weights():
                for dst, src in ((wqT_sb, wq_t), (wkT_sb, wk_t), (wvu_sb[:, :, 0:H], wv)):
                    sp.dma_start(dst, src.rearrange("(c p) n -> p c n", p=P)).then_inc(weights_in, 16)
                for dst, src in ((bq_sb, bq), (bk_sb, bk), (gamma_sb, gamma), (beta_sb, beta)):
                    sp.dma_start(dst[:, :], src.rearrange("(c p) -> p c", p=P),
                                 allow_slow_non_contiguous=True).then_inc(weights_in, 16)
                sp.dma_start(bv_sb[:, :], bv.rearrange("(a n) -> a n", a=1).broadcast_to([P, H])).then_inc(weights_in, 16)

            def attention(half, par):
                i = 2 * half + par
                if is_step(i + 2):
                    wait(sp, ln_ready, i + 1)
                    sp.dma_start(xa[par], x_s[bass.ds(QS * (i + 2), P), :, :]).then_inc(xa_in[par], 16)
                if is_step(i - 4):
                    n = i - 4
                    lo, hi = kept_rows(n)
                    wait(sp, ln2_ready, n + 1)
                    sp.dma_start(ln2_s[bass.ds(QS * n + lo, hi - lo), :, :], ln2[par][lo:hi]).then_inc(ln2_out[par], 16)
                if is_step(i - 1):
                    wait(sp, x2_ready, i - 2)
                    sp.dma_start(xr[1 - par], x_s[bass.ds(QS * (i - 1), P), :, :]).then_inc(xr_in[1 - par], 16)
                if is_step(i - 2):
                    n = i - 2
                    lo, hi = kept_rows(n)
                    wait(sp, x2_ready, n + 1)
                    sp.dma_start(x2_s[bass.ds(QS * n + lo, hi - lo), :, :], x2[par][lo:hi]).then_inc(x2_out[par], 16)

            attention(-1, 0)
            weights()
            attention(-1, 1)
            sp.dma_start(wquery_sb, w_query.rearrange("(u p) n -> p u n", p=P)).then_inc(fold_in, 16)
            sp.dma_start(keys_sb, keys_t).then_inc(fold_in, 16)
            rounds(sp, 0, STEPS + 3, attention, 6, A_TO)

            def load_piece(p_):
                wait(sp, table_split, p_ - 3)
                n, per = p_ % ST, CH * P // PIECE
                k, at = n // per, PIECE * (n % per)
                if p_ < ST:
                    sp.dma_start(piece[p_ % 4], down_t[k * P:(k + 1) * P, at:at + PIECE]).then_inc(table_in[p_ % 4], 16)
                else:
                    sp.dma_start(piece[p_ % 4].rearrange("p (c d) -> p c d", c=CS),
                                 up_c[CS * P * n:CS * P * (n + 1), :].rearrange("(c p) d -> p c d", p=P)
                                 ).then_inc(table_in[p_ % 4], 16)

            def store_lo(p_):
                sp.wait_ge(table_split, p_ + 1)
                sp.dma_start(up_lo_d[p_ % ST, :, :], up_lo[p_ % 4][:, :].bitcast(f32)).then_inc(lo_out[p_ % 4], 16)

            def load_lo(n, s_):
                wait(sp, y_done, n - 3)
                sp.dma_start(up_lo[s_ % 4][:, :].bitcast(f32), up_lo_d[s_, :, :]).then_inc(lo_in[s_ % 4], 16)

            def load_choices(g, par):
                wait(sp, bt_done, 2 * (g - 1))
                sp.dma_start(lnb[par][:, :, :], ln2_t[bass.ds(GT * g, GT), :].rearrange("(u p) d -> p u d", p=P)
                             ).then_inc(lnb_in[par], 16)

            sp.wait_ge(ln2_out[0], 32)
            sp.wait_ge(ln2_out[1], 16)
            load_choices(0, 0)
            for par in range(2):
                n = (STEPS + 1 - par) // 2
                sp.wait_ge(x2_out[par], 16 * n)
                sp.wait_ge(ln2_out[par], 16 * n)

            def load_products(g):
                wait(sp, rt_split, 2 * g)
                sp.dma_start(lnr[:, :, :], ln2_t[bass.ds(GT * g, GT), :].rearrange("(u p) d -> p u d", p=P)
                             ).then_inc(lnr_in, 16)

            def load_residual(g, at, stored):
                wait(sp, out_done[at], stored)
                sp.dma_start(xres[at][:, :, :], x2_t[bass.ds(GT * g, GT), :].rearrange("(u p) d -> p u d", p=P)
                             ).then_inc(xres_in[at], 16)

            def experts(half, par):
                r = 2 * half + par
                for s_ in range(ST):
                    if s_ == 0 and is_group(r - 1):
                        wait(sp, y_added, r)
                        sp.dma_start(out_t[bass.ds(GT * (r - 1), GT), :].rearrange("(u p) d -> p u d", p=P),
                                     xres[1 - par][:, :, :]).then_inc(out_done[1 - par], 16)
                    g, n = (r, s_ + 3) if s_ + 3 < ST else (r + 1, s_ + 3 - ST)
                    if is_group(r) and is_group(g):
                        load_lo(ST * g + n, n)
                    if s_ == 2 and is_group(r + 3):
                        load_choices(r + 3, 1 - par)
                    if s_ == 8 and is_group(r + 1):
                        load_residual(r + 1, 1 - par, 16 * (half + par))
                    if s_ == 15 and is_group(r + 2):
                        load_products(r + 2)

            for p_ in range(4):
                load_piece(p_)
            load_choices(1, 1)
            load_products(0)
            for p_ in range(4, ST):
                load_piece(p_)
            load_choices(2, 0)
            load_residual(0, 0, 0)
            for p_ in range(ST, 2 * ST):
                load_piece(p_)
                if p_ >= ST + 4:
                    store_lo(p_ - 4)
            for p_ in range(2 * ST - 4, 2 * ST):
                store_lo(p_)
            load_products(1)
            for i in range(4):
                sp.wait_ge(lo_out[i], 16 * 4)
            for n in range(3):
                load_lo(n, n)
            rounds(sp, 0, GROUPS, experts, B_FROM, B_TO)
            for par in range(2):
                sp.wait_ge(out_done[par], 16 * GROUPS // 2)

        @block.gpsimd
        def _(pool):
            g = nc.gpsimd
            g.memset(ident[:, :], 0.0).then_inc(const_step, 1)
            g.memset(band[:, :], 0.0).then_inc(const_step, 1)
            g.memset(valid[:, :], 1.0).then_inc(const_step, 1)
            g.iota(iota8[:, :], [[1, K]], base=0, channel_multiplier=0,
                   allow_small_or_imprecise_dtypes=True).then_inc(const_step, 1)
            g.iota(iota_rows[:, :, :], [[1, P], [0, PS]], base=0, channel_multiplier=0,
                   allow_small_or_imprecise_dtypes=True).then_inc(const_step, 1)
            g.iota(iota_cols[0:P // 2, :, :], [[1, 2 * HK], [0, PS]], base=0, channel_multiplier=0,
                   allow_small_or_imprecise_dtypes=True).then_inc(const_step, 1)
            pool.wait_ge(const_step, 6)
            g.iota(iota_cols[P // 2:P, :, :], [[1, 2 * HK], [0, PS]], base=-HK, channel_multiplier=0,
                   allow_small_or_imprecise_dtypes=True).then_inc(const_step, 1)
            pool.wait_ge(const_step, 7)
            g.affine_select(out=ident[:, :], in_=ident[:, :], compare_op=ALU.not_equal, fill=1.0,
                            base=0, pattern=[[-1, P]], channel_multiplier=1).then_inc(const_step, 1)
            g.affine_select(out=band[:, :], in_=band[:, :], compare_op=ALU.is_ge, fill=FAR,
                            base=W, pattern=[[-1, P]], channel_multiplier=1).then_inc(const_step, 1)
            g.affine_select(out=valid[:, 0:3:2], in_=valid[:, 0:3:2], compare_op=ALU.is_ge, fill=0.0,
                            base=P - W - 1, pattern=[[0, 2]], channel_multiplier=-1).then_inc(const_step, 1)
            pool.wait_ge(const_step, 10)
            g.affine_select(out=band[:, :], in_=band[:, :], compare_op=ALU.is_ge, fill=FAR,
                            base=W, pattern=[[1, P]], channel_multiplier=-1).then_inc(const_step, 1)
            g.affine_select(out=valid[:, 1:3], in_=valid[:, 1:3], compare_op=ALU.is_ge, fill=0.0,
                            base=-W, pattern=[[0, 2]], channel_multiplier=1).then_inc(const_step, 1)
            pool.wait_ge(const_step, 12)
            g.memset(ones[:, :], 1.0).then_inc(const_ready, 1)
            pool.wait_ge(weights_in, 16 * 8)

            def attention(half, par):
                i = 2 * half + par
                if is_step(i - 1):
                    xb = xr[1 - par]
                    wait(pool, xr_in[1 - par], 16 * (half + par))
                    g.tensor_tensor(xb, xb, bv_sb[:, :].unsqueeze(1).broadcast_to([P, NB, H]),
                                    ALU.add).then_inc(xb_ready, 1)
                n = i - 3
                if not is_step(n) or (known(n) and n >= STEPS - 2):
                    return
                l2 = ln2[1 - par].rearrange("p b d -> p (b d)")
                sq_f = sq.rearrange("p b d -> p (b d)")
                wait(pool, ln2_ready, n + 1)
                if known(n) and n == 0:
                    g.tensor_tensor(acc_edge[:, 0, 0, :], l2[:, 0:H], l2[:, H:2 * H], ALU.add).then_inc(stats_added, 1)
                    g.tensor_tensor(sq_f, l2, l2, ALU.mult).then_inc(sq_ready, 1)
                    wait(pool, sq_ready, 1)
                    g.tensor_tensor(acc_edge[:, 0, 1, :], sq_f[:, 0:H], sq_f[:, H:2 * H], ALU.add).then_inc(stats_added, 1)
                elif known(n) and n == 1:
                    g.tensor_copy(acc_mid[:, 0, :], l2).then_inc(stats_added, 1)
                    g.tensor_tensor(acc_mid[:, 1, :], l2, l2, ALU.mult).then_inc(stats_added, 1)
                else:
                    wait(pool, stats_added, 2 * n)
                    g.tensor_tensor(sq_f, l2, l2, ALU.mult).then_inc(sq_ready, 1)
                    g.tensor_tensor(acc_mid[:, 0, :], acc_mid[:, 0, :], l2, ALU.add).then_inc(stats_added, 1)
                    wait(pool, sq_ready, n)
                    g.tensor_tensor(acc_mid[:, 1, :], acc_mid[:, 1, :], sq_f, ALU.add).then_inc(stats_added, 1)

            rounds(pool, 1, STEPS + 1, attention, 6, A_TO)

            def experts(half, par):
                r = 2 * half + par
                for s_ in range(ST):
                    if is_group(r + 1) and s_ == SPLIT_AT[1]:
                        split_gates(2 * (r + 1) + 1, 1)
                    if is_group(r + 2) and s_ == SPLIT_AT[0]:
                        split_gates(2 * (r + 2), 0)
                    if is_group(r + 1):
                        gate_rows(ST * (r + 1) + s_, 2 * (r + 1) + s_ // TS, s_)
                    if s_ > 0 and is_group(r):
                        split_weights(ST * r + s_ - 1, s_ - 1)
                    if s_ == 0 and is_group(r - 1):
                        split_weights(ST * r - 1, ST - 1)
                    if known(r) and r == -2:
                        pool.wait_ge(table_rounded, s_ + 1)
                        at = slice(PIECE * s_, PIECE * (s_ + 1))
                        g.tensor_tensor(down_lo[:, at], piece[s_ % 4], down_hi[:, at], ALU.subtract).then_inc(table_split, 1)
                    if known(r) and r == GROUPS:
                        break

            def split_weights(d, s_):
                wait(pool, wgt_rounded, d + 1)
                wait(pool, y_done, d - 1)
                g.tensor_tensor(wgt_lo[s_ % 2][:, :, :], wgt[s_ % 2][:, :, :], wgt_hi[s_ % 2][:, :, :],
                                ALU.subtract).then_inc(wgt_split, 1)

            def gate_rows(q, n, s_):
                u, j = s_ // TS, PS * (s_ % TS)
                if s_ % TS == 0:
                    wait(pool, split_step, 3 * (n + 1))
                wait(pool, hits_ready, q + 1)
                wait(pool, gate_done, q - 1)
                m = DVE_PARTS
                shape = [P, 3 - m, 2 * HK, PS]
                g.tensor_tensor(cols_gate[s_ % 2][:, m:3, :, :], cols_hot[s_ % 2][:, :, :].unsqueeze(1).broadcast_to(shape),
                                gate3[u][:, m:3, j:j + PS].unsqueeze(2).broadcast_to(shape),
                                ALU.mult).then_inc(cols_ready, 1)

            def split_gates(n, u):
                wait(pool, cols_ready, TS * (n - 1))
                wait(pool, first_ready, TS * (n - 1))
                wait(pool, ct_read, n + 1)
                g.tensor_tensor(rest[:, :], gateT[u][:, :], gate3[u][:, 0, :], ALU.subtract).then_inc(split_step, 1)
                wait_apart(pool, split_step, 3 * n + 1)
                g.tensor_copy(gate3[u][:, 1, :], rest[:, :]).then_inc(split_step, 1)
                wait(pool, split_step, 3 * n + 2)
                g.tensor_tensor(gate3[u][:, 2, :], rest[:, :], gate3[u][:, 1, :], ALU.subtract).then_inc(split_step, 1)

            rounds(pool, -2, GROUPS, experts, B_FROM, B_TO)

        @block.tensor
        def _(pe):
            mm = nc.tensor.matmul
            pe.wait_ge(const_ready, 1)
            def weight_products():
                pe.wait_ge(weights_in, 16 * 8)
                for f in range(HC):
                    for m in range(HC):
                        last = mm(ps_w[:, f, :], wqT_sb[:, m, f * P:(f + 1) * P], wkT_sb[:, m, :],
                                  start=(m == 0), stop=(m == HC - 1))
                last.then_inc(a_done, 1)
                for ps, w, col in ((ps_c, wkT_sb, bq_sb), (ps_u, wqT_sb, bk_sb)):
                    for f in range(HC):
                        for m in range(HC):
                            last = mm(ps[:, f:f + 1], w[:, m, f * P:(f + 1) * P], col[:, m:m + 1],
                                      start=(m == 0), stop=(m == HC - 1))
                pe.wait_ge(bqk_ready, 1)
                for m in range(HC):
                    last = mm(ps_bqk, ones[:, :], bqk[:, m:m + 1], start=(m == 0), stop=(m == HC - 1))
                last.then_inc(weights_done, 1)

            def fold_keys(n):
                c, u0 = n // 2, NH * (n % 2)
                if n == 0:
                    pe.wait_ge(fold_in, 32)
                if n == 1:
                    pe.wait_ge(fold_copied, 1)
                for u in range(u0, u0 + NH):
                    last = mm(ps_fold[n][:, (u - u0) * NK:(u - u0 + 1) * NK], wquery_sb[:, u, c * P:(c + 1) * P],
                              keys_sb[:, u, :], start=True, stop=True)
                last.then_inc(fold_done, 1)

            def transposes(n):
                wait(pe, ln_ready, n + 1)
                for c in range(HC):
                    for b in range(NB):
                        last = nc.tensor.transpose(ps_t[:, c, b, :], ln[:, b, c * P:(c + 1) * P], ident[:, :])
                last.then_inc(t_done, 1)

            def attention(half, par):
                i = 2 * half + par
                if is_step(i):
                    wait(pe, lnT_ready, i + 1)
                    wait(pe, g_ready, i)
                    if known(i) and i == 0:
                        pe.wait_ge(a_ready, 1)
                    for m in range(HC):
                        for c in range(HC):
                            last = mm(ps_g[:, m, :], a_sb[:, c, m * P:(m + 1) * P],
                                      lnT[:, c, :, :].rearrange("p b t -> p (b t)"),
                                      start=(c == 0), stop=(c == HC - 1))
                    last.then_inc(g_done, 1)
                    wait(pe, v_ready, i)
                    if known(i) and i == 0:
                        pe.wait_ge(band_ready, 1)
                    for b in range(NB):
                        for c in range(HC):
                            last = mm(ps_v[b], lnT[:, c, b, :], wvu_sb[:, c, :], start=(c == 0), stop=(c == HC - 1))
                    last.then_inc(v_done, 1)
                if is_step(i - 1):
                    wait(pe, prT_ready, i - 1)
                    wait(pe, p_ready, i)
                    for b in range(NB):
                        last = nc.tensor.transpose(ps_pt[:, b, :], pr[:, b, :], ident[:, :])
                    last.then_inc(pt_done, 1)
                if known(i) and i in (0, 1):
                    fold_keys(i)
                if is_step(i):
                    wait(pe, g_ready, i + 1)
                    for b in range(NB):
                        for c in range(HC):
                            last = mm(ps_s[:, b, :], gT[:, c, b * P:(b + 1) * P], lnT[:, c, b, :],
                                      start=(c == 0), stop=(c == HC - 1))
                    last.then_inc(s_done, 1)
                if is_step(i + 1):
                    transposes(i + 1)
                if is_step(i - 1):
                    if known(i) and i == STEPS:
                        fold_keys(2)
                    wait(pe, prT_ready, i)
                    wait(pe, v_ready, i)
                    wait(pe, x2_ready, i - 1)
                    for b in range(NB):
                        last = mm(ps_o[:, b, :], prT[:, b, :], vu[1 - par][:, b, 0:H], start=True, stop=True)
                    last.then_inc(o_done, 1)

            attention(-1, 1)
            weight_products()
            rounds(pe, 0, STEPS, attention, A_FROM, A_TO)

            def column_sums(cols, kind, at, start, stop):
                for s in range(2):
                    for c in range(HC):
                        last = mm(ps_stat[s][c][:, 0:1], cols(s)[:, at + c * P:at + (c + 1) * P],
                                  valid[:, kind:kind + 1], start=start, stop=stop)
                return last

            pe.wait_ge(stats_added, 2)
            pe.wait_ge(fold_copied, 2)
            column_sums(lambda s: acc_edge[:, 0, s, :], 0, 0, True, False)
            pe.wait_ge(stats_added, 2 * (STEPS - 2))
            for b in range(NB):
                column_sums(lambda s: acc_mid[:, s, :], 2, b * H, False, False)
            pe.wait_ge(last_added, 1)
            column_sums(lambda s: acc_edge[:, 1, s, :], 2, 0, False, False)
            pe.wait_ge(last_added, 2)
            column_sums(lambda s: acc_edge[:, 2, s, :], 1, 0, False, True).then_inc(stat_done, 1)
            fold_keys(3)

            def choice_input(half, par, u):
                r = 2 * half + par
                n = 2 * (r + 2) + u
                if u == 0:
                    wait(pe, rt_split, 2 * (r + 1))
                    if known(r) and r == -1:
                        pe.wait_ge(ct_read, 1)
                    wait(pe, lnb_in[par], 16 * (half + 2))
                else:
                    wait(pe, ct_read, n - 1)
                for c in range(HC):
                    last = nc.tensor.transpose(ps_bt[:, c, :], lnb[par][:, u, c * P:(c + 1) * P], ident[:, :])
                last.then_inc(bt_done, 1)

            def choice_scores(n):
                wait(pe, bt_read, n + 1)
                wait(pe, topi_ready, UNITS * n)
                if known(n) and n == 0:
                    pe.wait_ge(fold_copied, 4)
                for m in range(2):
                    for c in range(HC):
                        last = mm(ps_sim[m][:, :], lnbT[:, c, :], fold[:, c, m * 512:(m + 1) * 512],
                                  start=(c == 0), stop=(c == HC - 1))
                    last.then_inc(sim_done, 1)

            def turn_codes(n):
                wait(pe, codes_ready, n + 1)
                wait(pe, tanh_ready, n + 1)
                wait(pe, bt_read, n + 2 if not known(n) else min(n + 2, TILES))
                if known(n) and n == TILES - 1:
                    pe.wait_ge(rt_split, TILES - 2)
                for a_ in range(3):
                    last = nc.tensor.transpose(ps_ct[:, a_, :], codes[:, a_, :, :].rearrange("p d s -> p (d s)"), ident[:, :])
                last.then_inc(ct_done, 1)

            def product_input(half, par, u):
                r = 2 * half + par
                n = 2 * (r + 1) + u
                if u == 0:
                    wait(pe, ct_read, n + 3 if not known(n) else min(n + 3, TILES))
                    wait(pe, lnr_in, 16 * (r + 2))
                else:
                    wait(pe, rt_split, n)
                for c in range(HC):
                    last = nc.tensor.transpose(ps_bt[:, c, :], lnr[:, u, c * P:(c + 1) * P], ident[:, :])
                last.then_inc(rt_done, 1)

            def add_up(r, s_):
                wait(pe, wgt_split, ST * r + s_ + 1)
                wait(pe, lo_in[s_ % 4], 16 * (4 * r + s_ // 4 + 1))
                if s_ == 0:
                    wait(pe, y_added, r)
                hi_p = up_hi[:, CS * H * s_:CS * H * (s_ + 1)].rearrange("p (c d) -> p c d", c=CS)
                lo_p = up_lo[s_ % 4][:, :].rearrange("p (c d) -> p c d", c=CS)
                terms = [(u, w[:, c, u * P:(u + 1) * P], t_[:, c, :]) for c in range(CS) for u in range(2)
                         for w, t_ in ((wgt_hi[s_ % 2], hi_p), (wgt_hi[s_ % 2], lo_p), (wgt_lo[s_ % 2], hi_p))]
                for m, (u, w, t_) in enumerate(terms):
                    last = mm(ps_y[:, u, :], w, t_, start=(s_ == 0 and m == 0),
                              stop=(s_ == ST - 1 and m == len(terms) - 1))
                last.then_inc(y_done, 1)

            def experts(half, par):
                r = 2 * half + par
                for s_ in range(ST):
                    u = s_ // TS
                    if is_group(r + 2) and s_ % TS == 0:
                        choice_input(half, par, u)
                    if is_group(r + 2) and s_ % TS == 1:
                        choice_scores(2 * (r + 2) + u)
                    if is_group(r + 1) and s_ in INPUT_AT:
                        product_input(half, par, INPUT_AT.index(s_))
                    if is_group(r):
                        d = ST * r + s_
                        if s_ == 0:
                            wait(pe, rt_split, 2 * (r + 1))
                            if known(r) and r == 0:
                                pe.wait_ge(table_split, ST)
                        wait(pe, gel_ready, d - 1)
                        for c in range(CS):
                            e = CS * s_ + c
                            terms = [(w[:, k, e, :], x_[par][:, k, :]) for k in range(HC)
                                     for w, x_ in ((hi4, ln_hi), (hi4, ln_lo), (lo4, ln_hi))]
                            for m, (w, x_) in enumerate(terms):
                                last = mm(ps_hid[s_ % 2][:, c * GT:(c + 1) * GT], w, x_,
                                          start=(m == 0), stop=(m == len(terms) - 1))
                        last.then_inc(hid_done, 1)
                    if is_group(r + 1):
                        q = ST * (r + 1) + s_
                        wait(pe, hits_ready, q + 1)
                        wait(pe, first_ready, q + 1)
                        wait(pe, cols_ready, q + 1)
                        wait(pe, gate_read, q - 1)
                        for j in range(PS):
                            for m in range(3):
                                last = mm(ps_gate[s_ % 2][:, j * 2 * HK:(j + 1) * 2 * HK], rows_hot[s_ % 2][:, :, j],
                                          cols_gate[s_ % 2][:, m, :, j], start=(m == 0), stop=(m == 2))
                        last.then_inc(gate_done, 1)
                    if s_ > 0 and is_group(r):
                        add_up(r, s_ - 1)
                    if s_ == 0 and is_group(r - 1):
                        add_up(r - 1, ST - 1)
                    if is_group(r + 1) and s_ == CODES_AT[1]:
                        turn_codes(2 * (r + 1) + 1)
                    if is_group(r + 2) and s_ == CODES_AT[0]:
                        turn_codes(2 * (r + 2))
                    if known(r) and r == GROUPS:
                        break

            rounds(pe, -2, GROUPS, experts, B_FROM, B_TO)

        @block.scalar
        def _(act):
            a = nc.scalar.activation
            def copy_products():
                act.wait_ge(a_done, 1)
                a(a_sb[:, :, :], ps_w, ACT.Copy, scale=SCALE)
                act.wait_ge(weights_done, 1)
                a(c_sb[:, :], ps_c, ACT.Copy, scale=SCALE)
                a(wvu_sb[:, :, H], ps_u, ACT.Copy, scale=SCALE).then_inc(a_ready, 1)

            def copy_fold(n):
                c, u0 = n // 2, NH * (n % 2)
                act.wait_ge(fold_done, n + 1)
                a(fold[:, c, u0 * NK:(u0 + NH) * NK], ps_fold[n][:, :], ACT.Copy).then_inc(fold_copied, 1)

            def attention(half, par):
                i = 2 * half + par
                if is_step(i):
                    wait(act, g_done, i + 1)
                    if known(i) and i == 0:
                        act.wait_ge(a_ready, 1)
                    for m in range(HC):
                        last = a(gT[:, m, :], ps_g[:, m, :], ACT.Identity, bias=c_sb[:, m:m + 1])
                    last.then_inc(g_ready, 1)
                    wait(act, v_done, i + 1)
                    wait(act, o_done, i - 1)
                    for b in range(NB):
                        last = a(vu[par][:, b, :], ps_v[b], ACT.Copy)
                    last.then_inc(v_ready, 1)
                if is_step(i - 1):
                    wait(act, pt_done, i)
                    a(prT, ps_pt, ACT.Copy).then_inc(prT_ready, 1)
                if known(i) and i in (0, 1):
                    copy_fold(i)
                if is_step(i + 1):
                    wait(act, s_done, i + 1)
                    wait(act, t_done, i + 2)
                    a(lnT, ps_t, ACT.Copy).then_inc(lnT_ready, 1)
                if is_step(i):
                    wait(act, nmax_ready, i + 1)
                    for b in range(NB):
                        last = a(pr[:, b, :], sm[:, b, :], ACT.Exp, bias=nmax[:, b:b + 1],
                                 accum_out=rsum[par][:, b:b + 1])
                    last.then_inc(p_ready, 1)

            attention(-1, 1)
            copy_products()
            rounds(act, 0, STEPS, attention, A_FROM, A_TO)
            copy_fold(2)
            copy_fold(3)

            def experts(half, par):
                r = 2 * half + par
                if known(r) and r == -1:
                    act.wait_ge(lnr_in, 16)
                for s_ in range(ST):
                    u = s_ // TS
                    if is_group(r + 2) and s_ % TS == 0:
                        n = 2 * (r + 2) + u
                        wait(act, bt_done, n + 1)
                        if known(n) and n == 0:
                            act.wait_ge(norm_ready, 1)
                        wait(act, sim_done, 2 * n)
                        for c in range(HC):
                            last = a(lnbT[:, c, :], ps_bt[:, c, :], ACT.Identity,
                                     bias=shift[:, c:c + 1], scale=factor[:, c:c + 1])
                        last.then_inc(bt_read, 1)
                    if is_group(r + 1) and s_ in INPUT_AT:
                        v_ = INPUT_AT.index(s_)
                        wait(act, rt_done, 2 * (r + 1) + v_ + 1)
                        wait(act, hid_done, ST * r)
                        a(ln_hi[1 - par][:, :, v_ * P:(v_ + 1) * P], ps_bt, ACT.Copy).then_inc(rt_read, 1)
                    if is_group(r):
                        d = ST * r + s_
                        wait(act, hid_done, d + 1)
                        wait(act, wgt_ready, d - 1)
                        a(gel[s_ % 2][:, :, :].rearrange("p c t -> p (c t)"), ps_hid[s_ % 2][:, :],
                          ACT.Gelu).then_inc(gel_ready, 1)
                        wait(act, wgt_ready, d + 1)
                        wait(act, y_done, d - 1)
                        a(wgt_hi[s_ % 2][:, :, :], wgt[s_ % 2][:, :, :], ACT.Copy).then_inc(wgt_rounded, 1)
                    if is_group(r + 1):
                        q, j = ST * (r + 1) + s_, PS * (s_ % TS)
                        wait(act, gate_done, q + 1)
                        wait(act, wgt_ready, ST * r + s_ + 1 if is_group(r) else 0)
                        blocks = grid[:, :, s_, :, :] if par == 0 else grid[:, s_, :, :, :]
                        a(blocks.rearrange("p a c t -> p t a c"),
                          ps_gate[s_ % 2][:, :].rearrange("p (t a c) -> p t a c", a=ST, c=CS), ACT.Copy).then_inc(gate_read, 1)
                    if is_group(r + 1) and s_ == CODES_AT[1]:
                        copy_codes(2 * (r + 1) + 1, 1)
                    if is_group(r + 2) and s_ == CODES_AT[0]:
                        copy_codes(2 * (r + 2), 0)
                    if known(r) and r < 0:
                        act.wait_ge(table_in[s_ % 4], 16 * (4 * (r + 2) + s_ // 4 + 1))
                        a((down_hi if r == -2 else up_hi)[:, PIECE * s_:PIECE * (s_ + 1)], piece[s_ % 4],
                          ACT.Copy).then_inc(table_rounded, 1)
                    if is_group(r + 2) and s_ % TS == TANH_AT:
                        n = 2 * (r + 2) + u
                        wait(act, best_ready, NH * (n + 1))
                        wait(act, ct_done, n)
                        a(codes[:, 2, :, :], best[:, :, :].rearrange("p h k -> p (h k)").unsqueeze(1).broadcast_to([P, 2, SEL]),
                          ACT.Tanh, scale=0.5).then_inc(tanh_ready, 1)

            def copy_codes(n, u):
                wait(act, ct_done, n + 1)
                wait(act, hits_ready, TS * (n - 1))
                wait(act, split_step, 3 * (n - 1))
                wait(act, first_ready, TS * (n - 1))
                for h in range(2):
                    side = slice(h * (P // 2), (h + 1) * (P // 2))
                    a(codesT[u][side, :, :], ps_ct[side, 0:2, h:P:2], ACT.Copy)
                    a(gateT[u][side, :], ps_ct[side, 2, h:P:2], ACT.Identity, bias=0.5, scale=0.5)
                    last = a(gate3[u][side, 0, :], ps_ct[side, 2, h:P:2], ACT.Identity, bias=0.5, scale=0.5)
                last.then_inc(ct_read, 1)

            rounds(act, -2, GROUPS - 1, experts, B_FROM, B_TO)

        @block.vector
        def _(dve):
            v = nc.vector
            v.memset(mv[:, :, :], 1.0).then_inc(mv_set, 1)
            dve.wait_ge(mv_set, 1)

            def root(var, y, sa, sb_, count, base, steps, between=()):
                fill = list(between)
                done = [0]

                def then(ins):
                    ins.then_inc(count, 1)
                    done[0] += 1
                    if fill:
                        fill.pop(0)()
                    wait(dve, count, base + done[0])

                then(v.tensor_scalar(y.bitcast(u32), var.bitcast(u32), -0.5, float(0x5F1FFFF9), ALU.mult, ALU.add))
                for n in range(steps):
                    ka, kb = (-0.703952253, 0.703952253 * 2.38924456) if n == 0 else (-0.5, 1.5)
                    then(v.tensor_tensor(sa, y, y, ALU.mult))
                    then(v.scalar_tensor_tensor(sb_, sa, ka, var, ALU.mult, ALU.mult))
                    then(v.scalar_tensor_tensor(y, sb_, kb, y, ALU.add, ALU.mult))
                for f in fill:
                    f()

            def last_sums(n, e):
                l2 = ln2[n % 2].rearrange("p b d -> p (b d)")
                sq_f = sq.rearrange("p b d -> p (b d)")

                def squares():
                    dve.wait_ge(stats_added, 2 * (STEPS - 2))
                    dve.wait_ge(ln2_ready, n + 1)
                    dve.wait_ge(last_added, e - 1) if e > 1 else None
                    v.tensor_tensor(sq_f, l2, l2, ALU.mult).then_inc(last_step, 1)

                def sums():
                    v.tensor_tensor(acc_edge[:, e, 0, :], l2[:, 0:H], l2[:, H:2 * H], ALU.add)

                def sums_of_squares():
                    dve.wait_ge(last_step, e)
                    v.tensor_tensor(acc_edge[:, e, 1, :], sq_f[:, 0:H], sq_f[:, H:2 * H], ALU.add).then_inc(last_added, 1)

                return [squares, sums, sums_of_squares]

            def attention(half, par):
                i = 2 * half + par
                fill = []

                def reciprocal():
                    wait(dve, p_ready, i - 1)
                    v.reciprocal(rcp[:, :], rsum[par][:, :]).then_inc(rcp_ready, 1)

                def output(b):
                    if b == 0:
                        wait(dve, rcp_ready, i - 1)
                        wait(dve, o_done, i - 1)
                        wait(dve, xb_ready, i - 1)
                        wait(dve, x2_out[par], 16 * (half - 1))
                    ins = v.scalar_tensor_tensor(x2[par][:, b, :], ps_o[:, b, :], rcp[:, b:b + 1],
                                                 xr[par][:, b, :], ALU.mult, ALU.add)
                    if b == NB - 1:
                        ins.then_inc(x2_ready, 1)

                def x2_stats(b):
                    if b == 0:
                        wait(dve, x2_ready, i - 1)
                    ins = v.bn_stats(bst[:, NB + b, :], x2[par][:, b, :])
                    if b == NB - 1:
                        ins.then_inc(x2_seen, 1)

                def xa_stats(b):
                    if b == 0:
                        wait(dve, xa_in[par], 16 * (half + 2))
                    ins = v.bn_stats(bst[:, b, :], xa[par][:, b, :])
                    if b == NB - 1:
                        ins.then_inc(xa_seen, 1)

                if is_step(i - 2):
                    fill += [reciprocal, lambda: output(0), lambda: output(1)]
                if is_step(i + 2):
                    fill += [lambda: xa_stats(0), lambda: xa_stats(1)]
                if is_step(i - 2):
                    fill += [lambda: x2_stats(0), lambda: x2_stats(1)]
                if known(i) and i == STEPS + 2:
                    fill += last_sums(STEPS - 2, 1)
                if is_step(i + 1) or is_step(i - 3):
                    wait(dve, veps_ready, i + 2)
                    root(veps[:, :], rstd[:, :], root_a[:, :], root_b[:, :], root_step, ROOT * (i + 1), 2, fill)
                else:
                    for f in fill:
                        f()
                if is_step(i + 1):
                    wait(dve, t_done, i + 1)
                    for b in range(NB):
                        last = v.tensor_scalar(ln[:, b, :], xa[1 - par][:, b, :], mv[:, b, 0:1], rstd[:, b:b + 1],
                                               ALU.subtract, ALU.mult)
                    last.then_inc(ln_ready, 1)
                if is_step(i - 3):
                    wait(dve, ln2_out[1 - par], 16 * (half - 2 + par))
                    wait(dve, stats_added, 2 * (i - 4) if not known(i) else 2 * min(i - 4, STEPS - 2))
                    for b in range(NB):
                        last = v.tensor_scalar(ln2[1 - par][:, b, :], x2[1 - par][:, b, :], mv[:, NB + b, 0:1],
                                               rstd[:, NB + b:NB + b + 1], ALU.subtract, ALU.mult)
                    last.then_inc(ln2_ready, 1)
                if is_step(i):
                    if known(i) and i == 0:
                        mask_constant()
                    wait(dve, s_done, i + 1)
                    wait(dve, v_ready, i + 1)
                    for b in range(NB):
                        last = v.scalar_tensor_tensor(sm[:, b, :], ps_s[:, b, :], vu[par][:, b, H:H + 1],
                                                      band[:, :], ALU.add, ALU.add)
                    last.then_inc(masked, 1)
                ahead, behind = is_step(i + 2), is_step(i - 2)
                if ahead or behind:
                    if is_step(i + 1):
                        wait(dve, ln_ready, i + 2)
                    if is_step(i - 3):
                        wait(dve, ln2_ready, i - 2)
                    if ahead:
                        wait(dve, xa_seen, i + 3)
                    if behind:
                        wait(dve, x2_seen, i - 1)
                    dve.nop(nofuse=True)
                    for b in range(0 if ahead else NB, 2 * NB if behind else NB):
                        last = v.bn_aggr(mv[:, b, :], bst[:, b, :])
                    last.then_inc(mv_ready, 1)
                if is_step(i):
                    wait(dve, masked, i + 1)
                    v.tensor_reduce(nmax[:, :], sm, AX.X, ALU.max, negate=True).then_inc(nmax_ready, 1)
                if ahead or behind:
                    wait(dve, mv_ready, i + 3)
                    v.tensor_scalar(veps[:, :], mv[:, :, 1], EPS, None, ALU.add).then_inc(veps_ready, 1)

            def mask_constant():
                dve.wait_ge(weights_done, 1)
                v.tensor_scalar(bqk_sb[:, :], ps_bqk, SCALE, None, ALU.mult).then_inc(bqk_scaled, 1)
                dve.wait_ge(bqk_scaled, 1)
                v.tensor_scalar(band[:, :], band[:, :], bqk_sb[:, :], None, ALU.add).then_inc(band_ready, 1)
                dve.wait_ge(band_ready, 1)

            ROOT = 7
            attention(-1, 0)
            attention(-1, 1)
            dve.wait_ge(const_ready, 1)
            dve.wait_ge(weights_in, 16 * 8)
            v.tensor_tensor(bqk[:, :], bq_sb[:, :], bk_sb[:, :], ALU.mult).then_inc(bqk_ready, 1)
            rounds(dve, 0, STEPS + 2, attention, 6, A_TO)

            for f in last_sums(STEPS - 1, 2):
                f()

            count = [0]

            def then(*group):
                count[0] += 1
                group[-1].then_inc(bs_step, 1)
                dve.wait_ge(bs_step, count[0])

            dve.wait_ge(stat_done, 1)
            then(*[v.tensor_scalar(mean[:, c:c + 1], ps_stat[0][c][:, 0:1], 1.0 / TOKENS, None, ALU.mult) for c in range(HC)],
                 *[v.tensor_scalar(ex2[:, c:c + 1], ps_stat[1][c][:, 0:1], 1.0 / TOKENS, EPS, ALU.mult, ALU.add) for c in range(HC)])
            then(v.tensor_tensor(msq, mean, mean, ALU.mult))
            then(v.tensor_tensor(bvar, ex2, msq, ALU.subtract))
            root(bvar, inv, bs_a, bs_b, bs_step, count[0], 3)
            count[0] += 10
            then(v.tensor_tensor(factor, inv, gamma_sb[:, :], ALU.mult))
            then(v.tensor_tensor(msq, mean, factor, ALU.mult))
            v.tensor_tensor(shift, beta_sb[:, :], msq, ALU.subtract).then_inc(norm_ready, 1)

            def best_keys(n, p, heads):
                if 0 in heads:
                    wait_apart(dve, sim_done, 2 * n + p + 1)
                for h in heads:
                    v.max(top[:, p * NH + h, :], ps_sim[p][:, h * NK:(h + 1) * NK]).then_inc(top_ready, 1)

            def name_keys(n, p):
                wait_apart(dve, top_ready, UNITS * n + NH * (p + 1))
                for h in range(NH):
                    v.max_index(topi[:, p * NH + h, :], top[:, p * NH + h, :],
                                ps_sim[p][:, h * NK:(h + 1) * NK]).then_inc(topi_ready, 1)

            def own(sem_, value):
                def then(*group):
                    group[-1].then_inc(sem_, 1)
                    wait_apart(dve, sem_, value)
                return then

            def best_pairs(n):
                first = top[:, 0:NH, :].unsqueeze(3).broadcast_to([P, NH, K, K])
                second = top[:, NH:UNITS, :].unsqueeze(2).broadcast_to([P, NH, K, K])
                wait(dve, tanh_ready, n)
                own(pair_ready, n + 1)(v.tensor_tensor(pair[:, :, :].rearrange("p h (i j) -> p h i j", i=K), first, second, ALU.add))
                for h in range(NH):
                    v.max(best[:, h, :], pair[:, h, :]).then_inc(best_ready, 1)

            def name_pairs(n):
                wait_apart(dve, best_ready, NH * (n + 1))
                own(besti_ready, n + 1)(*[v.max_index(besti[:, K * h:K * (h + 1)], best[:, h, :], pair[:, h, :]) for h in range(NH)])

                own(pos_ready, n + 1)(
                    v.tensor_scalar(pos[:, 0, :], besti[:, :], 3, None, ALU.logical_shift_right),
                    v.tensor_scalar(pos[:, 1, :], besti[:, :], K - 1, None, ALU.bitwise_and))

            def pick_keys(n):
                own(hot_ready, n + 1)(
                    v.tensor_tensor(hot[:, :, :, :], pos[:, :, :].unsqueeze(3).broadcast_to([P, 2, SEL, K]),
                                    iota8[:, :].unsqueeze(1).unsqueeze(1).broadcast_to([P, 2, SEL, K]), ALU.is_equal))

            def weigh_keys(n):
                wait(dve, topi_ready, UNITS * (n + 1))
                own(hotv_ready, n + 1)(
                    *[v.tensor_tensor(hot[:, p, :, :].rearrange("p (h k) m -> p h k m", h=NH),
                                      hot[:, p, :, :].rearrange("p (h k) m -> p h k m", h=NH),
                                      topi[:, p * NH:(p + 1) * NH, :].unsqueeze(2).broadcast_to([P, NH, K, K]),
                                      ALU.mult) for p in range(2)])

            def encode(n):
                own(part_ready, n + 1)(v.tensor_reduce(part[:, :, :], hot[:, :, :, :], AX.X, ALU.add))
                own(upper_ready, n + 1)(v.tensor_scalar(upper[:, :], part[:, 1, :], float(HK), None, ALU.is_ge))
                wait(dve, ct_done, n)
                twice = [x_.unsqueeze(1).broadcast_to([P, 2, SEL]) for x_ in (upper[:, :], part[:, 0, :], part[:, 1, :])]
                v.scalar_tensor_tensor(codes[:, 0, :, :], twice[0], float(NK), twice[1], ALU.mult, ALU.add)
                v.scalar_tensor_tensor(codes[:, 1, :, :], twice[0], -float(HK), twice[2], ALU.mult, ALU.add).then_inc(codes_ready, 1)

            def finish(r, half, par):
                wait(dve, y_done, ST * (r + 1))
                wait(dve, xres_in[par], 16 * (half + 1))
                v.tensor_tensor(xres[par][:, :, :], ps_y, xres[par][:, :, :], ALU.add).then_inc(y_added, 1)

            def one_hots(q, n, s_):
                u, j = s_ // TS, PS * (s_ % TS)
                if s_ % TS == 0:
                    wait(dve, ct_read, n + 1)
                wait(dve, gate_done, q - 1)
                wait(dve, cols_ready, q - 1)
                for hits, iota, a_ in ((rows_hot, iota_rows, 0), (cols_hot, iota_cols, 1)):
                    last = v.tensor_tensor(hits[s_ % 2][:, :, :], iota[:, :, :],
                                           codesT[u][:, a_, j:j + PS].unsqueeze(1).broadcast_to(iota.shape), ALU.is_equal)
                last.then_inc(hits_ready, 1)
            def first_parts(q, n, s_):
                u, j = s_ // TS, PS * (s_ % TS)
                if s_ % TS == 0:
                    wait(dve, split_step, 3 * n + 2)
                wait(dve, hits_ready, q + 1)
                m = DVE_PARTS
                shape = [P, m, 2 * HK, PS]
                v.tensor_tensor(cols_gate[s_ % 2][:, 0:m, :, :], cols_hot[s_ % 2][:, :, :].unsqueeze(1).broadcast_to(shape),
                                gate3[u][:, 0:m, j:j + PS].unsqueeze(2).broadcast_to(shape),
                                ALU.mult).then_inc(first_ready, 1)

            def experts(half, par):
                r = 2 * half + par
                for s_ in range(ST):
                    u = s_ // TS
                    if s_ == 1 and is_group(r - 1):
                        finish(r - 1, half if par else half - 1, 1 - par)
                    g, b = (r + 1, s_ + 1) if s_ < ST - 1 else (r + 2, 0)
                    if is_group(g):
                        one_hots(ST * g + b, 2 * g + b // TS, b)
                    if is_group(r):
                        d = ST * r + s_
                        wait(dve, gel_ready, d + 1)
                        if s_ == 0:
                            wait(dve, gate_read, ST * (r + 1))
                        wait(dve, wgt_split, d - 1)
                        blocks = grid[:, :, s_, :, :] if par == 0 else grid[:, s_, :, :, :]
                        tokens = "p c (b t) -> p c b t"
                        v.tensor_tensor(wgt[s_ % 2][:, :, :].rearrange(tokens, b=ST), gel[s_ % 2][:, :, :].rearrange(tokens, b=ST),
                                        blocks.rearrange("p b c t -> p c b t"), ALU.mult).then_inc(wgt_ready, 1)
                    if is_group(g):
                        first_parts(ST * g + b, 2 * g + b // TS, b)
                    if is_group(r + 1) and s_ in INPUT_AT:
                        v_ = INPUT_AT.index(s_)
                        wait(dve, rt_read, 2 * (r + 1) + v_ + 1)
                        v.tensor_tensor(ln_lo[1 - par][:, :, v_ * P:(v_ + 1) * P], ps_bt,
                                        ln_hi[1 - par][:, :, v_ * P:(v_ + 1) * P], ALU.subtract).then_inc(rt_split, 1)
                    if known(r) and r == -1:
                        if s_ >= 4:
                            dve.wait_ge(lo_out[s_ % 4], 16 * (s_ // 4))
                        dve.wait_ge(table_rounded, ST + s_ + 1)
                        v.tensor_tensor(up_lo[s_ % 4][:, :], piece[s_ % 4], up_hi[:, PIECE * s_:PIECE * (s_ + 1)],
                                        ALU.subtract).then_inc(table_split, 1)
                    n = 2 * (r + 2) + u - (1 if s_ % TS < 2 else 0)
                    if (s_ >= 2 and is_group(r + 2)) or (s_ < 2 and is_group(r + 1)):
                        choices[(s_ - 2) % TS](n)

            choices = (lambda n: (best_keys(n, 0, range(NH)), best_keys(n, 1, range(3))),
                       lambda n: (name_keys(n, 0), best_keys(n, 1, range(3, 5))),
                       lambda n: (best_keys(n, 1, range(5, NH)), name_keys(n, 1)),
                       best_pairs, name_pairs, pick_keys, weigh_keys, encode)
            rounds(dve, -2, GROUPS - 1, experts, B_FROM, B_TO)
            finish(GROUPS - 1, (GROUPS - 1) // 2, 1)


def kernel(L0_attn_sequence_output, L0_attn_Wq, L0_attn_bq, L0_attn_Wk, L0_attn_bk, L0_attn_Wv, L0_attn_bv,
           L0_ffn_bn_gamma, L0_ffn_bn_beta, L0_ffn_w_q, L0_ffn_keys_p, L0_ffn_down, L0_ffn_up):
    import numpy as np
    import concourse.bacc as bacc
    from concourse.bass_utils import run_bass_kernel_spmd

    keys = np.asarray(L0_ffn_keys_p)
    nh, nk, halves, kd = keys.shape

    def by_chunk(table):
        t = np.asarray(table)[:nk * nk].reshape(nk, 2, nk // 2, -1)
        return t.transpose(2, 1, 0, 3).reshape(nk * nk, -1)

    arrays = {
        "x": L0_attn_sequence_output, "wq_t": np.asarray(L0_attn_Wq).T, "bq": L0_attn_bq, "wk_t": np.asarray(L0_attn_Wk).T, "bk": L0_attn_bk,
        "wv": L0_attn_Wv, "bv": L0_attn_bv, "gamma": L0_ffn_bn_gamma, "beta": L0_ffn_bn_beta,
        "w_query": L0_ffn_w_q,
        "keys_t": keys.transpose(3, 2, 0, 1).reshape(kd, halves * nh, nk),
        "down_t": by_chunk(L0_ffn_down).T,
        "up_c": by_chunk(L0_ffn_up),
    }
    arrays = {n: np.ascontiguousarray(a) for n, a in arrays.items()}
    nc = bacc.Bacc("TRN2", target_bir_lowering=False, num_devices=1)
    args = [nc.dram_tensor(n, a.shape, mybir.dt.from_np(a.dtype), kind="ExternalInput").ap()
            for n, a in arrays.items()]
    shape = arrays["x"].shape
    out = nc.dram_tensor("out", shape, mybir.dt.float32, kind="ExternalOutput").ap()
    window_attention_peer_kernel(nc, *args, out)
    r = run_bass_kernel_spmd(nc, [arrays], core_ids=[0])
    return r.results[0]["out"]
```
